# Optimizing a Trainium2 kernel written in Bass

```python
import numpy as np
import jax
import jax.numpy as jnp

def _softmax(x, axis=-1):
    return jax.nn.softmax(x, axis=axis)

def _gelu(x):
    return jax.nn.gelu(x, approximate=True)

def _silu(x):
    return jax.nn.silu(x)

def _sigmoid(x):
    return jax.nn.sigmoid(x)

def _layernorm(x, axis=-1, eps=1e-05):
    m = jnp.mean(x, axis=axis, keepdims=True)
    v = jnp.var(x, axis=axis, keepdims=True)
    return (x - m) / jnp.sqrt(v + eps)

def _scatter_add(tgt, idx, src, axis=0):
    return tgt.at[idx].add(src)

def _segment_sum(src, seg, n):
    return jax.ops.segment_sum(src, seg, n)
kernel_name = 'mk_flamingo_gated_d1_seqx_r8_b05aad'

def setup_inputs(seed: int=0):
    np.random.seed(seed)
    _w = jnp.asarray

    def _rec_inputs():
        import jax
        import jax.numpy as jnp
        _rk = jax.random.key(seed)
        x = 7.22e-05 + 1 * jax.random.normal(jax.random.fold_in(_rk, 1), (4, 256, 128), jnp.float32)
        _lenS = 256 - jax.random.randint(jax.random.fold_in(_rk, 7), (4,), 0, max(1, 256 // 4) + 1, jnp.int32)
        _lenS2 = 1601 - jax.random.randint(jax.random.fold_in(_rk, 8), (4,), 0, max(1, 1601 // 4) + 1, jnp.int32)
        _ctx_1024P = jax.random.normal(jax.random.fold_in(_rk, 11), (4, 16, 128), jnp.float32)
        _ctx_1024c = jax.random.dirichlet(jax.random.fold_in(_rk, 511), 0.3 * jnp.ones((16,), jnp.float32), (4, 1601))
        _ctx_1024t = jnp.einsum('bsk,bkd->bsd', _ctx_1024c, _ctx_1024P)
        _ctx_1024t = _ctx_1024t * jax.lax.rsqrt(jnp.mean(jnp.square(_ctx_1024t)) + 1e-12) * 0.953939
        ctx_1024 = 4.13588e-05 + 0.999923 * (_ctx_1024t + 0.3 * jax.random.normal(jax.random.fold_in(_rk, 611), (4, 1601, 128), jnp.float32))
        _g = jax.random.normal(jax.random.fold_in(_rk, 9001), (2, 1), jnp.float32)
        _g = jnp.sign(_g) * jnp.maximum(jnp.abs(_g), 1.0) + (_g == 0) * 1.0
        g_xattn = _g[0]
        g_ffn = _g[1]
        return (x, ctx_1024, g_xattn, g_ffn)
    x, ctx_1024, g_xattn, g_ffn = _rec_inputs()

    def _L0_xattn_setup():
        import jax, jax.numpy as jnp
        import numpy as np
        HIDDEN = 128
        key = jax.random.key(seed)
        kq, kk, kwq, kwk, kwv = jax.random.split(key, 5)
        B, S, D = (4, 256, HIDDEN)
        query = jax.random.normal(kq, (B, S, D), dtype=jnp.float32)
        key_t = jax.random.normal(kk, (B, S, D), dtype=jnp.float32)
        scale = 1.0 / np.sqrt(D)
        Wq = jax.random.normal(kwq, (D, D), dtype=jnp.float32) * scale
        Wk = jax.random.normal(kwk, (D, D), dtype=jnp.float32) * scale
        Wv = jax.random.normal(kwv, (D, D), dtype=jnp.float32) * scale
        return {'query': query, 'key': key_t, 'Wq': Wq, 'Wk': Wk, 'Wv': Wv}
    _L0_xattn_all = _L0_xattn_setup()
    _L0_xattn_in = {k: v for k, v in _L0_xattn_all.items() if k in ('Wq', 'Wk', 'Wv')}
    del _L0_xattn_all

    def _L0_ffn_setup():
        import jax, jax.numpy as jnp
        import numpy as np
        B, S, H = (2, 128, 128)
        E, F = (16, 64)
        G, TOPK_G, TOPK = (4, 2, 4)
        N_SHARED = 2
        ROUTE_SCALE = 1.0
        FS = N_SHARED * F

        def _gate(x, w_gate):
            T = x.shape[0]
            scores = jax.nn.sigmoid(x @ w_gate.T)
            sv = scores.reshape(T, G, E // G)
            group_scores = jax.lax.top_k(sv, 2)[0].sum(-1)
            top_groups = jax.lax.top_k(group_scores, TOPK_G)[1]
            allowed = jnp.zeros((T, G), dtype=bool).at[jnp.arange(T)[:, None], top_groups].set(True)
            masked = jnp.where(allowed[:, :, None], sv, -jnp.inf).reshape(T, E)
            _, idx = jax.lax.top_k(masked, TOPK)
            w = jnp.take_along_axis(scores, idx, axis=1)
            w = w / (w.sum(-1, keepdims=True) + 1e-06) * ROUTE_SCALE
            return (w, idx)

        def _swiglu(x, w1, w3, w2):
            return jax.nn.silu(x @ w1.T) * (x @ w3.T) @ w2.T
        key = jax.random.key(seed)
        ks = jax.random.split(key, 8)
        scale = 0.02
        return {'hidden_states': jax.random.normal(ks[0], (B, S, H), dtype=jnp.float32), 'w_gate': jax.random.normal(ks[1], (E, H), dtype=jnp.float32) * scale, 'w1_e': jax.random.normal(ks[2], (E, F, H), dtype=jnp.float32) * scale, 'w3_e': jax.random.normal(ks[3], (E, F, H), dtype=jnp.float32) * scale, 'w2_e': jax.random.normal(ks[4], (E, H, F), dtype=jnp.float32) * scale, 'w1_s': jax.random.normal(ks[5], (FS, H), dtype=jnp.float32) * scale, 'w3_s': jax.random.normal(ks[6], (FS, H), dtype=jnp.float32) * scale, 'w2_s': jax.random.normal(ks[7], (H, FS), dtype=jnp.float32) * scale}
    _L0_ffn_all = _L0_ffn_setup()
    _L0_ffn_in = {k: v for k, v in _L0_ffn_all.items() if k in ('w_gate', 'w1_e', 'w3_e', 'w2_e', 'w1_s', 'w3_s', 'w2_s')}
    del _L0_ffn_all
    return {'x': x, 'ctx_1024': ctx_1024, 'g_xattn': g_xattn, 'g_ffn': g_ffn, 'L0_xattn_Wq': _L0_xattn_in['Wq'], 'L0_xattn_Wk': _L0_xattn_in['Wk'], 'L0_xattn_Wv': _L0_xattn_in['Wv'], 'L0_ffn_w_gate': _L0_ffn_in['w_gate'], 'L0_ffn_w1_e': _L0_ffn_in['w1_e'], 'L0_ffn_w3_e': _L0_ffn_in['w3_e'], 'L0_ffn_w2_e': _L0_ffn_in['w2_e'], 'L0_ffn_w1_s': _L0_ffn_in['w1_s'], 'L0_ffn_w3_s': _L0_ffn_in['w3_s'], 'L0_ffn_w2_s': _L0_ffn_in['w2_s']}

def reference(x, ctx_1024, g_xattn, g_ffn, L0_xattn_Wq, L0_xattn_Wk, L0_xattn_Wv, L0_ffn_w_gate, L0_ffn_w1_e, L0_ffn_w3_e, L0_ffn_w2_e, L0_ffn_w1_s, L0_ffn_w3_s, L0_ffn_w2_s):
    import jax
    import jax.numpy as jnp

    def _L0_xattn_ref(query, key, Wq, Wk, Wv):
        import jax, jax.numpy as jnp
        import numpy as np
        HIDDEN = 128
        Q = jnp.einsum('bsd,ed->bse', query, Wq)
        K = jnp.einsum('bsd,ed->bse', key, Wk)
        V = jnp.einsum('bsd,ed->bse', key, Wv)
        alpha = jnp.einsum('bqd,bkd->bqk', Q, K)
        alpha = jax.nn.softmax(alpha, axis=2)
        out = jnp.einsum('bqk,bkd->bqd', alpha, V)
        return out

    def _L0_ffn_ref(hidden_states, w_gate, w1_e, w3_e, w2_e, w1_s, w3_s, w2_s):
        import jax, jax.numpy as jnp
        import numpy as np
        B, S, H = (2, 128, 128)
        E, F = (16, 64)
        G, TOPK_G, TOPK = (4, 2, 4)
        N_SHARED = 2
        ROUTE_SCALE = 1.0
        FS = N_SHARED * F

        def _gate(x, w_gate):
            T = x.shape[0]
            scores = jax.nn.sigmoid(x @ w_gate.T)
            sv = scores.reshape(T, G, E // G)
            group_scores = jax.lax.top_k(sv, 2)[0].sum(-1)
            top_groups = jax.lax.top_k(group_scores, TOPK_G)[1]
            allowed = jnp.zeros((T, G), dtype=bool).at[jnp.arange(T)[:, None], top_groups].set(True)
            masked = jnp.where(allowed[:, :, None], sv, -jnp.inf).reshape(T, E)
            _, idx = jax.lax.top_k(masked, TOPK)
            w = jnp.take_along_axis(scores, idx, axis=1)
            w = w / (w.sum(-1, keepdims=True) + 1e-06) * ROUTE_SCALE
            return (w, idx)

        def _swiglu(x, w1, w3, w2):
            return jax.nn.silu(x @ w1.T) * (x @ w3.T) @ w2.T
        shape = hidden_states.shape
        x = hidden_states.reshape(-1, H)
        weights, idx = _gate(x, w_gate)
        combine = (jax.nn.one_hot(idx, E, dtype=x.dtype) * weights[..., None]).sum(1)
        g = jax.nn.silu(jnp.einsum('th,efh->tef', x, w1_e))
        u = jnp.einsum('th,efh->tef', x, w3_e)
        routed = jnp.einsum('tef,ehf,te->th', g * u, w2_e, combine)
        shared = _swiglu(x, w1_s, w3_s, w2_s)
        return (routed + shared).reshape(shape)
    x = x + jnp.tanh(g_xattn[0]) * _L0_xattn_ref(_layernorm(x, axis=-1), ctx_1024, L0_xattn_Wq, L0_xattn_Wk, L0_xattn_Wv)
    x = x + jnp.tanh(g_ffn[0]) * _L0_ffn_ref(_layernorm(x, axis=-1), L0_ffn_w_gate, L0_ffn_w1_e, L0_ffn_w3_e, L0_ffn_w2_e, L0_ffn_w1_s, L0_ffn_w3_s, L0_ffn_w2_s)
    return x

_drawn_inputs = setup_inputs


def setup_inputs(seed=0):
    import zlib

    import numpy as np

    out = dict(_drawn_inputs(seed))
    spreads = {}
    factors = {'L0_ffn_w_gate': 8.0,
     'L0_ffn_w1_e': 8.0,
     'L0_ffn_w3_e': 8.0,
     'L0_ffn_w2_e': 8.0,
     'L0_ffn_w1_s': 8.0,
     'L0_ffn_w3_s': 8.0,
     'L0_ffn_w2_s': 8.0}
    for name, (base, spread) in spreads.items():
        noise = np.random.default_rng([zlib.crc32(name.encode()), seed]).standard_normal(out[name].shape)
        drawn = base * np.exp(spread * noise) if base else spread * noise
        out[name] = jnp.asarray(drawn.astype(out[name].dtype))
    for name, factor in factors.items():
        out[name] = (out[name] * factor).astype(out[name].dtype)
    return out
```

```python
from contextlib import ExitStack

import concourse.bass as bass
from concourse import mybir

P = 128
D = 128
BATCHES = 4
SEQ = 256
KEYS = 1601
EXPERTS = 16
GROUPS = 4
HIDDEN = 64
EPS = 1e-5

QT = SEQ // P
TILES = BATCHES * QT
TOKENS = BATCHES * SEQ
KT = -(-KEYS // P)
FULL_KT = KEYS // P
TAIL = KEYS - FULL_KT * P
KEYS_EVEN = KEYS + KEYS % 2
PAIRS = -(-KT // 2)
BANK = 512
CHUNKS = ((0, BANK), (BANK, 2 * BANK), (2 * BANK, KEYS))
NCH = len(CHUNKS)
HALVES = 2
HTOK = TOKENS // HALVES
HTILES = TILES // HALVES
FT = EXPERTS * HIDDEN // P + 1
WCOLS = FT * P
STEPS = HALVES * FT
PT_RING = 3

ALU = mybir.AluOpType
ACT = mybir.ActivationFunctionType
AX = mybir.AxisListType
F32 = mybir.dt.float32
F32R = mybir.dt.float32r


def build(nc, x, ctxT, ctxN, ctxTail, wq, wk, wvT, wgT, w1T, w3T, w2T, g_xattn, g_ffn, outT):
    with ExitStack() as stack:
        def sb(name, shape, dt=F32):
            return stack.enter_context(nc.sbuf_tensor(name, shape, dt))

        def sem(name):
            return stack.enter_context(nc.semaphore(name))

        ident = sb("ident", [P, P])
        neghalf = sb("neghalf", [P, TILES])
        x_sb = sb("x_sb", [P, TILES, D])
        wq_sb = sb("wq_sb", [P, D])
        wk_sb = sb("wk_sb", [P, D])
        wv_sb = sb("wv_sb", [P, D])
        wqk = sb("wqk", [P, D])
        gates = sb("gates", [P, 2])
        tgates = sb("tgates", [P, 2])
        stats = sb("stats", [P, TILES, 6])
        meanvar = sb("meanvar", [P, TILES, 2])
        vareps = sb("vareps", [P, TILES])
        rstd = sb("rstd", [P, TILES])
        xn = sb("xn", [P, TILES, D])
        xnT = sb("xnT", [P, TOKENS])
        q_hi = sb("q_hi", [P, TOKENS], F32R)
        q_lo = sb("q_lo", [P, TOKENS], F32R)
        cT = sb("cT", [P, 2, KEYS])
        cT_hi = sb("cT_hi", [P, 2, KEYS_EVEN], F32R)
        cT_lo = sb("cT_lo", [P, 2, KEYS_EVEN], F32R)
        cN = sb("cN", [P, 2, KT * D])
        cN_hi = sb("cN_hi", [P, 2, KT * D], F32R)
        cN_lo = sb("cN_lo", [P, 2, KT * D], F32R)
        probs = sb("probs", [P, 2, QT, KEYS])
        pT_hi = sb("pT_hi", [P, PT_RING, BANK], F32R)
        pT_lo = sb("pT_lo", [P, PT_RING, BANK], F32R)
        chunk_max = sb("chunk_max", [P, TILES, NCH])
        neg_max = sb("neg_max", [P, TILES])
        chunk_sum = sb("chunk_sum", [P, TILES, NCH])
        row_sum = sb("row_sum", [P, TILES])
        inv_sum = sb("inv_sum", [P, TILES])
        attn_scale = sb("attn_scale", [P, TILES])
        oT = sb("oT", [P, SEQ])
        x1 = sb("x1", [P, TILES, D])
        stats2 = sb("stats2", [P, TILES, 6])
        meanvar2 = sb("meanvar2", [P, TILES, 2])
        vareps2 = sb("vareps2", [P, TILES])
        rstd2 = sb("rstd2", [P, TILES])
        y = sb("y", [P, QT, D])
        x1T = sb("x1T", [P, TOKENS])
        yT_hi = sb("yT_hi", [P, TOKENS], F32R)
        yT_lo = sb("yT_lo", [P, TOKENS], F32R)
        wg = sb("wg", [P, EXPERTS])
        wg_hi = sb("wg_hi", [P, EXPERTS], F32R)
        wg_lo = sb("wg_lo", [P, EXPERTS], F32R)
        w_raw = sb("w_raw", [P, 2, WCOLS])
        w_hi = sb("w_hi", [P, 3, WCOLS], F32R)
        w_lo = sb("w_lo", [P, 3, WCOLS], F32R)
        expneg = sb("expneg", [P, TILES, EXPERTS])
        comb = sb("comb", [P, HTILES, P])
        combT = sb("combT", [P, TOKENS], F32R)
        sel = sb("sel", [P, EXPERTS * HIDDEN], F32R)
        r_den = sb("r_den", [P, HTILES, EXPERTS])
        r_sig = sb("r_sig", [P, HTILES, EXPERTS])
        r_pair = sb("r_pair", [P, HTILES * GROUPS, 6])
        r_group = sb("r_group", [P, HTILES, GROUPS])
        r_ge = sb("r_ge", [P, HTILES, GROUPS, GROUPS])
        r_gt = sb("r_gt", [P, HTILES, GROUPS, GROUPS])
        r_lower = sb("r_lower", [P, HTILES, GROUPS, GROUPS])
        r_higher = sb("r_higher", [P, HTILES, GROUPS, GROUPS])
        r_rank = sb("r_rank", [P, HTILES, GROUPS])
        r_allow = sb("r_allow", [P, HTILES, GROUPS])
        r_off = sb("r_off", [P, HTILES, GROUPS])
        r_masked = sb("r_masked", [P, HTILES, EXPERTS])
        r_top = sb("r_top", [P, HTILES, 8])
        r_above = sb("r_above", [P, HTILES, EXPERTS])
        r_tie = sb("r_tie", [P, HTILES, EXPERTS])
        r_carry = sb("r_carry", [P, HTILES, EXPERTS])
        r_count = sb("r_count", [P, HTILES, EXPERTS])
        r_nabove = sb("r_nabove", [P, HTILES])
        r_w = sb("r_w", [P, HTILES, EXPERTS])
        r_wsum = sb("r_wsum", [P, HTILES])
        r_winv = sb("r_winv", [P, HTILES])

        early = probs[:, 0, :, :].rearrange("p a b -> p (a b)")
        silu = [early[:, k * BANK:(k + 1) * BANK] for k in (0, 1)]
        gated = [early[:, k * BANK:(k + 1) * BANK] for k in (2, 3)]
        z = [early[:, k * BANK:(k + 1) * BANK] for k in (4, 5)]
        z_hi, z_lo = pT_hi, pT_lo
        out_sb = xnT
        sel_raw = xn[:, :, :].rearrange("p a b -> p (a b)")

        ps_s = stack.enter_context(nc.psum_tensor("ps_s", [P, 4, BANK], F32))
        ps_t = stack.enter_context(nc.psum_tensor("ps_t", [P, 2, BANK], F32))
        ps_o = stack.enter_context(nc.psum_tensor("ps_o", [P, BANK], F32))
        ps_m = stack.enter_context(nc.psum_tensor("ps_m", [P, BANK], F32))
        scores = ps_s[:, :, :].rearrange("p a b -> p (a b)")
        h1 = [ps_s[:, 0, :], ps_s[:, 1, :]]
        h3 = [ps_s[:, 2, :], ps_s[:, 3, :]]
        spread = [ps_t[:, 0, :], ps_t[:, 1, :]]
        acc = [ps_o, ps_m]

        l_x0, l_x, l_wq, l_wv, l_wg, l_gate = (sem(n) for n in ("l_x0", "l_x", "l_wq", "l_wv", "l_wg", "l_gate"))
        l_cT = [sem(f"l_cT{k}") for k in range(2)]
        l_cN = [sem(f"l_cN{k}") for k in range(2)]
        l_w = [sem(f"l_w{k}") for k in range(3)]
        s_fill = sem("s_fill")
        s_ident = sem("s_ident")
        s_tailz = sem("s_tailz")
        s_consts = sem("s_consts")
        s_sel = sem("s_sel")
        s_tg = sem("s_tg")
        s_wqk = sem("s_wqk")
        s_wqk_sb = sem("s_wqk_sb")
        s_var = sem("s_var")
        s_rstd = sem("s_rstd")
        s_xn = sem("s_xn")
        s_xT = sem("s_xT")
        s_xT_sb = sem("s_xT_sb")
        s_q = sem("s_q")
        s_qhi = sem("s_qhi")
        s_qlo = sem("s_qlo")
        s_cThi = sem("s_cThi")
        s_cTlo = sem("s_cTlo")
        s_cNhi = sem("s_cNhi")
        s_cNlo = sem("s_cNlo")
        s_score = sem("s_score")
        s_cmax = sem("s_cmax")
        s_max = sem("s_max")
        s_exp = sem("s_exp")
        s_turn = sem("s_turn")
        s_pThi = sem("s_pThi")
        s_pTlo = sem("s_pTlo")
        s_pv = sem("s_pv")
        s_oT = sem("s_oT")
        s_attn = sem("s_attn")
        s_scale = sem("s_scale")
        s_x1 = sem("s_x1")
        s_var2 = sem("s_var2")
        s_rstd2 = sem("s_rstd2")
        s_y = sem("s_y")
        s_yT = sem("s_yT")
        s_yTact = sem("s_yTact")
        s_yTlo = sem("s_yTlo")
        s_st = sem("s_st")
        s_whi = sem("s_whi")
        s_wlo = sem("s_wlo")
        s_wghi = sem("s_wghi")
        s_wglo = sem("s_wglo")
        s_logit = sem("s_logit")
        s_expneg = sem("s_expneg")
        s_route = sem("s_route")
        s_comb = sem("s_comb")
        s_combT = sem("s_combT")
        s_combT_sb = sem("s_combT_sb")
        s_up = sem("s_up")
        s_spread = sem("s_spread")
        s_silu = sem("s_silu")
        s_gated = sem("s_gated")
        s_z = sem("s_z")
        s_zhi = sem("s_zhi")
        s_zlo = sem("s_zlo")
        s_down = sem("s_down")
        s_out = sem("s_out")
        l_out = sem("l_out")

        NGROUP = 2
        group_tiles = (range(0, QT), range(QT, TILES))

        def pairs_of(b, qt):
            first = PAIRS * (b - 1)
            if b == 0:
                return [], []
            if qt == 0:
                return [first], [first + 1, first + 2]
            return [first + 3], [first + 4, first + 5, first + 6]

        def pair_tiles(g):
            p = g % PAIRS
            return [t for t in (2 * p, 2 * p + 1) if t < KT]

        def rows(t):
            return P if t < FULL_KT else TAIL

        def chunk_of(t):
            return min((t * P + rows(t) - 1) // BANK, NCH - 1)

        def is_shared(i):
            return i % FT == 0

        def w_tile(i):
            t = FT - 1 if is_shared(i) else i % FT - 1
            return slice(t * P, (t + 1) * P)

        def routed_steps(i):
            return i + 1 - (i // FT + 1)

        block = stack.enter_context(nc.Block())

        @block.sync
        def _(sp):
            sp.dma_start(x_sb[:, 0:QT, :], x[:, 0:QT * D]).then_inc(l_x0, 16)
            sp.dma_start(wq_sb[:, :], wq).then_inc(l_wq, 16)
            sp.dma_start(wk_sb[:, :], wk).then_inc(l_wq, 16)
            sp.dma_start(x_sb[:, QT:TILES, :], x[:, QT * D:TILES * D]).then_inc(l_x, 16)
            sp.wait_ge(s_tailz, 1)

            def load_ctx(b):
                if b >= 1:
                    sp.dma_start(cT[:, b % 2, :], ctxT[b]).then_inc(l_cT[b % 2], 16)
                sp.dma_start(cN[:, b % 2, 0:FULL_KT * D], ctxN[b]).then_inc(l_cN[b % 2], 16)
                sp.dma_start(cN[0:TAIL, b % 2, FULL_KT * D:KT * D], ctxTail[b]).then_inc(l_cN[b % 2], 16)

            load_ctx(0)
            load_ctx(1)
            sp.dma_start(wv_sb[:, :], wvT).then_inc(l_wv, 16)
            sp.dma_start(wg[:, :], wgT).then_inc(l_wg, 16)
            for k, w in enumerate((w1T, w3T)):
                sp.dma_start(w_raw[:, k, :], w).then_inc(l_w[k], 16)
            for b in range(2, BATCHES):
                sp.wait_ge(s_cThi, NCH * (b - 1))
                sp.wait_ge(s_cTlo, NCH * (b - 1))
                sp.wait_ge(s_cNhi, b - 1)
                sp.wait_ge(s_cNlo, b - 1)
                load_ctx(b)
            sp.wait_ge(s_wlo, 1)
            sp.dma_start(w_raw[:, 0, :], w2T).then_inc(l_w[2], 16)
            for n in range(2 * HALVES):
                sp.wait_ge(s_out, n + 1)
                w = HTOK // 2
                sp.dma_start(outT[:, n * w:(n + 1) * w], out_sb[:, n * w:(n + 1) * w]).then_inc(l_out, 16)
            sp.wait_ge(l_out, 16 * 2 * HALVES)

        @block.gpsimd
        def _(pool):
            nc.gpsimd.memset(ident[:, :], 1.0).then_inc(s_fill, 1)
            nc.gpsimd.memset(neghalf[:, :], -0.5).then_inc(s_fill, 1)
            pool.wait_ge(s_fill, 2)
            nc.gpsimd.affine_select(out=ident[:, :], in_=ident[:, :], compare_op=ALU.is_equal, fill=0.0,
                                    base=0, pattern=[[-1, P]], channel_multiplier=1).then_inc(s_ident, 1)

            def rsqrt(var, out, tiles, ready, n, done):
                pool.wait_ge(ready, n)
                a, b = tiles[0], tiles[-1] + 1
                nc.gpsimd.tensor_tensor(out[:, a:b], var[:, a:b], neghalf[:, a:b], ALU.pow).then_inc(done, 1)

            for k, tiles in enumerate(group_tiles):
                rsqrt(vareps, rstd, tiles, s_var, k + 1, s_rstd)

            def cN_low(b):
                pool.wait_ge(s_cNhi, b + 1)
                if b >= 2:
                    pool.wait_ge(s_pv, PAIRS * (b - 1))
                nc.gpsimd.tensor_tensor(cN_lo[:, b % 2, :], cN[:, b % 2, :], cN_hi[:, b % 2, :].bitcast(F32),
                                        ALU.subtract).then_inc(s_cNlo, 1)

            def cT_low(b):
                for c, (a, e) in enumerate(CHUNKS):
                    pool.wait_ge(s_cThi, NCH * b + c + 1)
                    if b >= 2:
                        pool.wait_ge(s_score, NCH * QT * (b - 1))
                    nc.gpsimd.tensor_tensor(cT_lo[:, b % 2, a:e], cT[:, b % 2, a:e],
                                            cT_hi[:, b % 2, a:e].bitcast(F32), ALU.subtract).then_inc(s_cTlo, 1)

            def w_low(k):
                pool.wait_ge(s_whi, k + 1)
                nc.gpsimd.tensor_tensor(w_lo[:, k, :], w_raw[:, k % 2, :], w_hi[:, k, :].bitcast(F32),
                                        ALU.subtract).then_inc(s_wlo, 1)

            def batch_rsqrt2(j):
                rsqrt(vareps2, rstd2, range(QT * j, QT * j + QT), s_var2, j + 1, s_rstd2)

            cT_low(1)
            cN_low(0)
            sel3 = sel_raw.rearrange("p (e f) -> p e f", f=HIDDEN)
            pool.wait_ge(s_xT, NGROUP)
            nc.gpsimd.memset(sel_raw, 0.0).then_inc(s_fill, 1)
            pool.wait_ge(s_fill, 3)
            nc.gpsimd.affine_select(out=sel3, in_=sel3, compare_op=ALU.not_equal, fill=1.0, base=0,
                                    pattern=[[-1, EXPERTS], [0, HIDDEN]], channel_multiplier=1).then_inc(s_fill, 1)
            pool.wait_ge(s_fill, 4)
            nc.gpsimd.affine_select(out=sel3, in_=sel3, compare_op=ALU.not_equal, fill=1.0, base=-EXPERTS,
                                    pattern=[[-1, EXPERTS], [0, HIDDEN]], channel_multiplier=1).then_inc(s_fill, 1)
            cN_low(1)
            cT_low(2)
            w_low(0)
            cN_low(2)
            batch_rsqrt2(0)
            cT_low(3)
            w_low(1)
            cN_low(3)
            batch_rsqrt2(1)
            w_low(2)
            batch_rsqrt2(2)
            batch_rsqrt2(3)
            for i in range(STEPS):
                pool.wait_ge(s_zhi, i + 1)
                if i >= PT_RING:
                    pool.wait_ge(s_down, i - PT_RING + 1)
                nc.gpsimd.tensor_tensor(z_lo[:, i % PT_RING, :], z[i % 2], z_hi[:, i % PT_RING, :].bitcast(F32),
                                        ALU.subtract).then_inc(s_zlo, 1)

        @block.scalar
        def _(act):
            act.dma_start(cT[:, 0, :], ctxT[0]).then_inc(l_cT[0], 16)
            act.dma_start(gates[:, 0:1], g_xattn.broadcast_to([P, 1])).then_inc(l_gate, 16)
            act.dma_start(gates[:, 1:2], g_ffn.broadcast_to([P, 1])).then_inc(l_gate, 16)

            def cT_high(b, c):
                a, e = CHUNKS[c]
                act.wait_ge(l_cT[b % 2], 16 * (b // 2 + 1))
                if b >= 2:
                    act.wait_ge(s_score, NCH * QT * (b - 1))
                nc.scalar.copy(cT_hi[:, b % 2, a:e], cT[:, b % 2, a:e]).then_inc(s_cThi, 1)

            def move_x(k):
                a, e = group_tiles[k][0] * P, (group_tiles[k][-1] + 1) * P
                w = min(e - a, BANK)
                act.wait_ge(s_xT, k + 1)
                nc.scalar.copy(xnT[:, a:a + w], ps_t[:, 0, 0:w]).then_inc(s_xT_sb, 1)
                if e - a > BANK:
                    nc.scalar.copy(xnT[:, a + w:e], ps_t[:, 1, 0:e - a - w]).then_inc(s_xT_sb, 1)

            def q_high(k):
                a, e = group_tiles[k][0] * P, (group_tiles[k][-1] + 1) * P
                w = min(e - a, BANK)
                act.wait_ge(s_q, k + 1)
                nc.scalar.copy(q_hi[:, a:a + w], ps_o[:, 0:w]).then_inc(s_qhi, 1)
                if e - a > BANK:
                    nc.scalar.copy(q_hi[:, a + w:e], ps_m[:, 0:e - a - w]).then_inc(s_qhi, 1)

            def exponential(b, qt, c):
                s = QT * b + qt
                a, e = CHUNKS[c]
                act.wait_ge(s_max, s + 1)
                if b >= 2:
                    act.wait_ge(s_turn, PAIRS * (b - 1))
                nc.scalar.activation(probs[:, b % 2, qt, a:e], scores[:, a:e], ACT.Exp, bias=neg_max[:, s:s + 1],
                                     accum_out=chunk_sum[:, s, c:c + 1]).then_inc(s_exp, 1)

            def high(g):
                w = len(pair_tiles(g)) * SEQ
                r = rows(pair_tiles(g)[-1])
                act.wait_ge(s_turn, g + 1)
                if g >= PT_RING:
                    act.wait_ge(s_pv, g - PT_RING + 1)
                nc.scalar.copy(pT_hi[0:r, g % PT_RING, 0:w], ps_t[0:r, g % 2, 0:w]).then_inc(s_pThi, 1)

            def move_o(j):
                act.wait_ge(s_pv, PAIRS * (j + 1))
                if j >= 1:
                    act.wait_ge(s_attn, j)
                nc.scalar.copy(oT[:, :], ps_o[:, 0:SEQ]).then_inc(s_oT, 1)

            def move_y(j):
                a = SEQ * j
                act.wait_ge(s_yT, j + 1)
                nc.scalar.copy(yT_hi[:, a:a + SEQ], ps_m[:, 0:SEQ]).then_inc(s_yTact, 1)
                nc.scalar.copy(x1T[:, a:a + SEQ], ps_m[:, SEQ:2 * SEQ]).then_inc(s_yTact, 1)

            def exp_logits(j):
                act.wait_ge(s_logit, j + 1)
                nc.scalar.activation(expneg[:, QT * j:QT * j + QT, :].rearrange("p a b -> p (a b)"),
                                     ps_m[:, 0:QT * EXPERTS], ACT.Exp, scale=-1.0).then_inc(s_expneg, 1)

            act.wait_ge(s_wqk, 1)
            nc.scalar.copy(wqk[:, :], ps_m[:, 0:D]).then_inc(s_wqk_sb, 1)
            cT_high(0, 0)
            move_x(0)
            q_high(0)
            cT_high(0, 1)
            cT_high(0, 2)
            act.wait_ge(l_gate, 32)
            nc.scalar.activation(tgates[:, :], gates[:, :], ACT.Tanh).then_inc(s_tg, 1)
            for b in range(BATCHES + 1):
                for qt in range(QT):
                    before, after = pairs_of(b, qt)
                    if b >= 3 and qt == 0:
                        exp_logits(b - 3)
                    if b == 0 and qt == 0:
                        move_x(1)
                    for g in before:
                        high(g)
                    if b >= 2 and qt == 0:
                        move_o(b - 2)
                    for c in range(NCH):
                        if b < BATCHES:
                            exponential(b, qt, c)
                        if c < len(after):
                            high(after[c])
                        if b == 0 and qt == 0 and c == 0:
                            q_high(1)
                        if qt == 0 and b < BATCHES - 1:
                            cT_high(b + 1, c)
                    if b >= 2 and qt == 1:
                        move_y(b - 2)
            exp_logits(2)
            move_o(3)

            def silu_of(i):
                act.wait_ge(s_up, i + 1)
                if i == 0:
                    act.wait_ge(s_turn, PAIRS * (BATCHES - 1))
                if i >= 2:
                    act.wait_ge(s_gated, i - 1)
                nc.scalar.activation(silu[i % 2], h1[i % 2], ACT.Silu).then_inc(s_silu, 1)

            def z_high(i):
                if is_shared(i):
                    act.wait_ge(s_gated, i + 1)
                else:
                    act.wait_ge(s_z, routed_steps(i))
                if i == 0:
                    act.wait_ge(s_pv, PAIRS * BATCHES)
                if i >= PT_RING:
                    act.wait_ge(s_down, i - PT_RING + 1)
                nc.scalar.copy(z_hi[:, i % PT_RING, :], z[i % 2]).then_inc(s_zhi, 1)

            for i in range(STEPS + 1):
                if i < STEPS:
                    silu_of(i)
                if i >= 1:
                    z_high(i - 1)
                if i == 0:
                    act.wait_ge(s_combT, 1)
                    nc.scalar.copy(combT[:, 0:HTOK], ps_m[:, :]).then_inc(s_combT_sb, 1)
                if i == 5:
                    move_y(3)
                if i == 6:
                    exp_logits(3)
                if i == FT:
                    act.wait_ge(s_combT, 2)
                    nc.scalar.copy(combT[:, HTOK:TOKENS], ps_m[:, :]).then_inc(s_combT_sb, 1)

        @block.vector
        def _(dve):
            steps = [0]

            def link(ins):
                steps[0] += 1
                ins.then_inc(s_st, 1)
                dve.wait_ge(s_st, steps[0])

            routed = [0]

            def route(ins):
                routed[0] += 1
                ins.then_inc(s_route, 1)
                dve.wait_ge(s_route, routed[0])

            def norm_stats(src, st, mv, var, tiles, done):
                for t in tiles:
                    ins = nc.vector.bn_stats(st[:, t, :], src[:, t, :])
                link(ins)
                for t in tiles:
                    ins = nc.vector.bn_aggr(mv[:, t, :], st[:, t, :])
                link(ins)
                a, b = tiles[0], tiles[-1] + 1
                nc.vector.tensor_scalar(var[:, a:b], mv[:, a:b, 1], EPS, None, ALU.add).then_inc(done, 1)

            def norm_x(k):
                dve.wait_ge(s_rstd, k + 1)
                for t in group_tiles[k]:
                    ins = nc.vector.tensor_scalar(xn[:, t, :], x_sb[:, t, :], meanvar[:, t, 0:1], rstd[:, t:t + 1],
                                                  ALU.subtract, ALU.mult)
                    ins.then_inc(s_xn, 1)

            def q_low(k):
                a, e = group_tiles[k][0] * P, (group_tiles[k][-1] + 1) * P
                w = min(e - a, BANK)
                dve.wait_ge(s_qhi, k + 1)
                ins = nc.vector.tensor_tensor(q_lo[:, a:a + w], ps_o[:, 0:w], q_hi[:, a:a + w].bitcast(F32),
                                              ALU.subtract)
                if e - a > BANK:
                    dve.wait_ge(s_qhi, 3)
                    ins = nc.vector.tensor_tensor(q_lo[:, a + w:e], ps_m[:, 0:e - a - w],
                                                  q_hi[:, a + w:e].bitcast(F32), ALU.subtract)
                ins.then_inc(s_qlo, 1)

            def cT_low0(c):
                a, e = CHUNKS[c]
                dve.wait_ge(s_cThi, c + 1)
                nc.vector.tensor_tensor(cT_lo[:, 0, a:e], cT[:, 0, a:e], cT_hi[:, 0, a:e].bitcast(F32),
                                        ALU.subtract).then_inc(s_cTlo, 1)

            def cN_high(b):
                dve.wait_ge(l_cN[b % 2], 32 * (b // 2 + 1))
                if b >= 2:
                    dve.wait_ge(s_pv, PAIRS * (b - 1))
                nc.vector.tensor_copy(cN_hi[:, b % 2, :], cN[:, b % 2, :]).then_inc(s_cNhi, 1)

            def w_high(k):
                dve.wait_ge(l_w[k], 16)
                nc.vector.tensor_copy(w_hi[:, k, :], w_raw[:, k % 2, :]).then_inc(s_whi, 1)

            def chunk_maximum(b, qt, c):
                s = QT * b + qt
                a, e = CHUNKS[c]
                dve.wait_ge(s_score, NCH * s + c + 1)
                nc.vector.tensor_reduce(chunk_max[:, s, c:c + 1], scores[:, a:e], AX.X, ALU.max).then_inc(s_cmax, 1)

            def maximum(b, qt):
                s = QT * b + qt
                dve.wait_ge(s_cmax, NCH * (s + 1))
                nc.vector.tensor_reduce(neg_max[:, s:s + 1], chunk_max[:, s, :], AX.X, ALU.max,
                                        negate=True).then_inc(s_max, 1)

            def low(g):
                w = len(pair_tiles(g)) * SEQ
                r = rows(pair_tiles(g)[-1])
                dve.wait_ge(s_pThi, g + 1)
                if g >= PT_RING:
                    dve.wait_ge(s_pv, g - PT_RING + 1)
                nc.vector.tensor_tensor(pT_lo[0:r, g % PT_RING, 0:w], ps_t[0:r, g % 2, 0:w],
                                        pT_hi[0:r, g % PT_RING, 0:w].bitcast(F32), ALU.subtract).then_inc(s_pTlo, 1)

            def residual(j):
                a, e = QT * j, QT * j + QT
                dve.wait_ge(s_exp, NCH * e)
                link(nc.vector.tensor_reduce(row_sum[:, a:e], chunk_sum[:, a:e, :], AX.X, ALU.add))
                link(nc.vector.reciprocal(inv_sum[:, a:e], row_sum[:, a:e]))
                dve.wait_ge(s_tg, 1)
                link(nc.vector.tensor_scalar(attn_scale[:, a:e], inv_sum[:, a:e], tgates[:, 0:1], None, ALU.mult))
                dve.wait_ge(s_attn, j + 1)
                for t in range(a, e):
                    ins = nc.vector.scalar_tensor_tensor(out=x1[:, t, :], in0=ps_m[:, (t - a) * D:(t - a + 1) * D],
                                                         scalar=attn_scale[:, t:t + 1], in1=x_sb[:, t, :],
                                                         op0=ALU.mult, op1=ALU.add)
                    ins.then_inc(s_x1, 1)
                dve.wait_ge(s_x1, e)
                norm_stats(x1, stats2, meanvar2, vareps2, range(a, e), s_var2)

            def norm_y(j):
                a = QT * j
                dve.wait_ge(s_rstd2, j + 1)
                if j >= 1:
                    dve.wait_ge(s_yT, j)
                for t in range(a, a + QT):
                    nc.vector.tensor_scalar(y[:, t - a, :], x1[:, t, :], meanvar2[:, t, 0:1], rstd2[:, t:t + 1],
                                            ALU.subtract, ALU.mult).then_inc(s_y, 1)

            def yT_low(j):
                a = SEQ * j
                dve.wait_ge(s_yTact, 2 * (j + 1))
                nc.vector.tensor_tensor(yT_lo[:, a:a + SEQ], ps_m[:, 0:SEQ], yT_hi[:, a:a + SEQ].bitcast(F32),
                                        ALU.subtract).then_inc(s_yTlo, 1)

            def bc(v, n):
                return v.unsqueeze(len(v.shape)).broadcast_to(list(v.shape) + [n])

            def router(h, part):
                if part == 0:
                    dve.wait_ge(s_expneg, QT * (h + 1))
                    route(nc.vector.tensor_scalar(r_den[:], expneg[:, HTILES * h:HTILES * (h + 1), :], 1.0, None,
                                                  ALU.add))
                    route(nc.vector.reciprocal(r_sig[:], r_den[:]))
                    sg = r_sig[:].rearrange("p t (g m) -> p (t g) m", g=GROUPS)
                    nc.vector.tensor_tensor(r_pair[:, :, 0:2], sg[:, :, 0:2], sg[:, :, 2:4], ALU.add)
                    nc.vector.tensor_tensor(r_pair[:, :, 2:4], sg[:, :, 0:4:2], sg[:, :, 1:4:2], ALU.add)
                    nc.vector.tensor_tensor(r_pair[:, :, 4:5], sg[:, :, 0:1], sg[:, :, 3:4], ALU.add)
                    route(nc.vector.tensor_tensor(r_pair[:, :, 5:6], sg[:, :, 1:2], sg[:, :, 2:3], ALU.add))
                    route(nc.vector.tensor_reduce(r_group[:].rearrange("p t g -> p (t g)"), r_pair[:], AX.X, ALU.max))
                if part == 1:
                    dve.wait_ge(s_consts, 1)
                    mine = r_group[:].unsqueeze(3).broadcast_to([P, HTILES, GROUPS, GROUPS])
                    other = r_group[:].unsqueeze(2).broadcast_to([P, HTILES, GROUPS, GROUPS])
                    nc.vector.tensor_tensor(r_gt[:], other, mine, ALU.is_gt)
                    route(nc.vector.tensor_tensor(r_ge[:], other, mine, ALU.is_ge))
                    nc.vector.tensor_tensor(r_gt[:], r_gt[:], r_higher[:], ALU.mult)
                    route(nc.vector.tensor_tensor(r_ge[:], r_ge[:], r_lower[:], ALU.mult))
                    route(nc.vector.tensor_tensor(r_gt[:], r_gt[:], r_ge[:], ALU.add))
                    route(nc.vector.tensor_reduce(r_rank[:], r_gt[:], AX.X, ALU.add))
                    nc.vector.tensor_scalar(r_allow[:], r_rank[:], 1.5, None, ALU.is_lt)
                    route(nc.vector.tensor_scalar(r_off[:], r_rank[:], 1.5, -1.0, ALU.is_gt, ALU.mult))
                    n = EXPERTS // GROUPS
                    sg = r_sig[:].rearrange("p t (g m) -> p (t g) m", g=GROUPS)
                    mk = r_masked[:].rearrange("p t (g m) -> p (t g) m", g=GROUPS)
                    route(nc.vector.tensor_tensor(mk, sg, bc(r_allow[:].rearrange("p t g -> p (t g)"), n), ALU.mult))
                    route(nc.vector.tensor_tensor(mk, mk, bc(r_off[:].rearrange("p t g -> p (t g)"), n), ALU.add))
                if part == 2:
                    for t in range(HTILES):
                        ins = nc.vector.max(r_top[:, t, :], r_masked[:, t, :])
                    route(ins)
                    fourth = r_top[:, :, 3:4].broadcast_to([P, HTILES, EXPERTS])
                    nc.vector.tensor_tensor(r_above[:], r_masked[:], fourth, ALU.is_gt)
                    route(nc.vector.tensor_tensor(r_tie[:], r_masked[:], fourth, ALU.is_equal))
                    nc.vector.tensor_reduce(r_nabove[:], r_above[:], AX.X, ALU.add)
                    route(nc.vector.tensor_tensor_scan(r_count[:].rearrange("p t e -> p (t e)"),
                                                       r_carry[:].rearrange("p t e -> p (t e)"),
                                                       r_tie[:].rearrange("p t e -> p (t e)"), 0.0,
                                                       ALU.mult, ALU.add))
                    route(nc.vector.tensor_tensor(r_count[:], r_count[:], bc(r_nabove[:], EXPERTS), ALU.add))
                    route(nc.vector.scalar_tensor_tensor(out=r_tie[:].rearrange("p t e -> p (t e)"),
                                                         in0=r_count[:].rearrange("p t e -> p (t e)"), scalar=4.5,
                                                         in1=r_tie[:].rearrange("p t e -> p (t e)"),
                                                         op0=ALU.is_lt, op1=ALU.mult))
                    route(nc.vector.tensor_tensor(r_above[:], r_above[:], r_tie[:], ALU.add))
                if part == 3:
                    route(nc.vector.tensor_tensor(r_w[:], r_above[:], r_sig[:], ALU.mult))
                    route(nc.vector.tensor_reduce(r_wsum[:], r_w[:], AX.X, ALU.add))
                    route(nc.vector.tensor_scalar(r_wsum[:], r_wsum[:], 1e-6, None, ALU.add))
                    route(nc.vector.reciprocal(r_winv[:], r_wsum[:]))
                    route(nc.vector.tensor_tensor(r_w[:], r_w[:], bc(r_winv[:], EXPERTS), ALU.mult))
                    if h >= 1:
                        dve.wait_ge(s_combT, h)
                    route(nc.vector.tensor_copy(comb[:, :, 0:EXPERTS].bitcast(F32R), r_w[:]))
                    nc.vector.tensor_tensor(comb[:, :, EXPERTS:2 * EXPERTS], r_w[:], comb[:, :, 0:EXPERTS],
                                            ALU.subtract).then_inc(s_comb, 1)

            nc.vector.memset(cN[TAIL // 32 * 32:P, :, FULL_KT * D:KT * D], 0.0).then_inc(s_tailz, 1)
            nc.vector.memset(cT_hi[:, :, KEYS:KEYS_EVEN].bitcast(F32), 0.0).then_inc(s_tailz, 1)
            nc.vector.memset(cT_lo[:, :, KEYS:KEYS_EVEN].bitcast(F32), 0.0).then_inc(s_tailz, 1)
            dve.wait_ge(l_x0, 16)
            norm_stats(x_sb, stats, meanvar, vareps, group_tiles[0], s_var)
            norm_x(0)
            dve.wait_ge(l_x, 16)
            norm_stats(x_sb, stats, meanvar, vareps, group_tiles[1], s_var)
            cT_low0(0)
            q_low(0)
            cT_low0(1)
            cT_low0(2)
            norm_x(1)
            nc.vector.memset(comb[:], 0.0)
            nc.vector.memset(r_lower[:], 0.0)
            nc.vector.memset(r_higher[:], 0.0)
            link(nc.vector.memset(r_carry[:], 1.0))
            nc.vector.memset(r_carry[:, :, 0:1], 0.0)
            for g in range(1, GROUPS):
                nc.vector.memset(r_lower[:, :, g, 0:g], 1.0)
                ins = nc.vector.memset(r_higher[:, :, g - 1, g:GROUPS], 1.0)
            ins.then_inc(s_consts, 1)

            for b in range(BATCHES + 1):
                for qt in range(QT):
                    before, after = pairs_of(b, qt)
                    if b < BATCHES:
                        chunk_maximum(b, qt, 0)
                        chunk_maximum(b, qt, 1)
                    for g in before:
                        low(g)
                    if b >= 2 and qt == 1:
                        norm_y(b - 2)
                    if b < BATCHES:
                        chunk_maximum(b, qt, 2)
                        maximum(b, qt)
                    if b == 0 and qt == 0:
                        q_low(1)
                    if b >= 2 and qt == 0 and b < BATCHES:
                        for g in after[:1]:
                            low(g)
                        residual(b - 2)
                        for g in after[1:]:
                            low(g)
                    else:
                        for n, g in enumerate(after):
                            low(g)
                            if b == BATCHES and qt == 0:
                                residual(2) if n == 0 else router(0, 0)
                            if b == BATCHES and qt == 1:
                                router(0, n + 1)
                    if b >= 2 and qt == 1:
                        yT_low(b - 2)
                    if qt == 0 and b < BATCHES:
                        cN_high(b)
                    if qt == 1 and b < 3:
                        w_high(b)
                    if b == 1 and qt == 1:
                        dve.wait_ge(l_wg, 16)
                        nc.vector.tensor_copy(wg_hi[:, :], wg[:, :]).then_inc(s_wghi, 1)
                        dve.wait_ge(s_wghi, 1)
                        nc.vector.tensor_tensor(wg_lo[:, :], wg[:, :], wg_hi[:, :].bitcast(F32),
                                                ALU.subtract).then_inc(s_wglo, 1)
                        dve.wait_ge(s_fill, 5)
                        nc.vector.tensor_copy(sel[:, :], sel_raw).then_inc(s_sel, 1)

            def gate(i):
                dve.wait_ge(s_silu, i + 1)
                if i >= 2:
                    dve.wait_ge(s_zhi, i - 1)
                    dve.wait_ge(s_zlo, i - 1)
                to = z if is_shared(i) else gated
                nc.vector.tensor_tensor(to[i % 2], silu[i % 2], h3[i % 2], ALU.mult).then_inc(s_gated, 1)
                if not is_shared(i):
                    dve.wait_ge(s_gated, i + 1)
                    dve.wait_ge(s_spread, routed_steps(i))
                    nc.vector.tensor_tensor(z[i % 2], gated[i % 2], spread[i % 2], ALU.mult).then_inc(s_z, 1)

            def finish(h):
                dve.wait_ge(s_down, FT * (h + 1))
                w = HTOK // 2
                for n in range(2):
                    a = h * HTOK + n * w
                    nc.vector.scalar_tensor_tensor(out=out_sb[:, a:a + w], in0=acc[h][:, n * w:(n + 1) * w],
                                                   scalar=tgates[:, 1:2], in1=x1T[:, a:a + w],
                                                   op0=ALU.mult, op1=ALU.add).then_inc(s_out, 1)

            for i in range(STEPS):
                gate(i)
                if i == 1:
                    residual(3)
                if i == 3:
                    norm_y(3)
                if i == 5:
                    yT_low(3)
                if i == 7:
                    router(1, 0)
                    router(1, 1)
                if i == 8:
                    router(1, 2)
                    router(1, 3)
                if i == FT + 2:
                    finish(0)
            finish(1)

        @block.tensor
        def _(pe):
            def product(out, parts):
                lh, ll, rh, rl = parts
                nc.tensor.matmul(out, lh, rh, start=True, stop=False)
                nc.tensor.matmul(out, lh, rl, start=False, stop=False)
                return nc.tensor.matmul(out, ll, rh, start=False, stop=True)

            def turn_x(k):
                tiles = group_tiles[k]
                if k >= 1:
                    pe.wait_ge(s_xT_sb, 1)
                for n, t in enumerate(tiles):
                    pe.wait_ge(s_xn, t + 1)
                    ins = nc.tensor.transpose(ps_t[:, n // 4, n % 4 * P:(n % 4 + 1) * P], xn[:, t, :], ident[:, :])
                ins.then_inc(s_xT, 1)

            def query(k):
                a, e = group_tiles[k][0] * P, (group_tiles[k][-1] + 1) * P
                w = min(e - a, BANK)
                pe.wait_ge(s_xT_sb, 1 if k == 0 else 3)
                if k == 1:
                    pe.wait_ge(s_qlo, 1)
                ins = nc.tensor.matmul(ps_o[:, 0:w], wqk[:, :], xnT[:, a:a + w], start=True, stop=True)
                if e - a > BANK:
                    ins = nc.tensor.matmul(ps_m[:, 0:e - a - w], wqk[:, :], xnT[:, a + w:e], start=True, stop=True)
                ins.then_inc(s_q, 1)

            def score(b, qt, c):
                s = QT * b + qt
                a, e = CHUNKS[c]
                if s >= 1:
                    pe.wait_ge(s_exp, NCH * (s - 1) + c + 1)
                if c == 0 and qt == 0:
                    pe.wait_ge(s_qhi, 1 if b == 0 else 3)
                    pe.wait_ge(s_qlo, 1 if b == 0 else 2)
                pe.wait_ge(s_cThi, NCH * b + c + 1)
                pe.wait_ge(s_cTlo, NCH * b + c + 1)
                q = slice(s * P, (s + 1) * P)
                if s == 0 and c == 0:
                    pe.wait_ge(s_tailz, 3)
                for k in range(a, e, BANK):
                    m = slice(k, min(k + BANK, KEYS_EVEN))
                    ins = product(scores[:, m], (q_hi[:, q], q_lo[:, q], cT_hi[:, b % 2, m], cT_lo[:, b % 2, m]))
                ins.then_inc(s_score, 1)

            def turn(g):
                b = g // PAIRS
                if g < 2:
                    pe.wait_ge(s_xT_sb, 3)
                else:
                    pe.wait_ge(s_pTlo, g - 1)
                for n, t in enumerate(pair_tiles(g)):
                    pe.wait_ge(s_exp, NCH * (QT * b + 1) + chunk_of(t) + 1)
                    for qt in range(QT):
                        o = (n * QT + qt) * P
                        ins = nc.tensor.transpose(ps_t[0:rows(t), g % 2, o:o + P],
                                                  probs[:, b % 2, qt, t * P:t * P + rows(t)], ident[:, :])
                ins.then_inc(s_turn, 1)

            def weigh(g):
                b = g // PAIRS
                if g % PAIRS == 0:
                    pe.wait_ge(s_cNhi, b + 1)
                    pe.wait_ge(s_cNlo, b + 1)
                    if b == 0:
                        pe.wait_ge(s_qlo, 2)
                    else:
                        pe.wait_ge(s_oT, b)
                pe.wait_ge(s_pThi, g + 1)
                pe.wait_ge(s_pTlo, g + 1)
                for n, t in enumerate(pair_tiles(g)):
                    r = rows(t)
                    c_hi, c_lo = (v[0:r, b % 2, t * D:(t + 1) * D] for v in (cN_hi, cN_lo))
                    p_hi, p_lo = (v[0:r, g % PT_RING, n * SEQ:(n + 1) * SEQ] for v in (pT_hi, pT_lo))
                    nc.tensor.matmul(ps_o[:, 0:SEQ], c_hi, p_hi, start=(t == 0), stop=False)
                    nc.tensor.matmul(ps_o[:, 0:SEQ], c_lo, p_hi, start=False, stop=False)
                    ins = nc.tensor.matmul(ps_o[:, 0:SEQ], c_hi, p_lo, start=False, stop=(t == KT - 1))
                ins.then_inc(s_pv, 1)

            def attend(j):
                pe.wait_ge(s_oT, j + 1)
                if j == 0:
                    pe.wait_ge(l_wv, 16)
                    pe.wait_ge(s_qlo, 2)
                elif j < BATCHES - 1:
                    pe.wait_ge(s_expneg, j)
                else:
                    pe.wait_ge(s_combT_sb, 1)
                for qt in range(QT):
                    ins = nc.tensor.matmul(ps_m[:, qt * D:(qt + 1) * D], oT[:, qt * P:(qt + 1) * P], wv_sb[:, :],
                                           start=True, stop=True)
                ins.then_inc(s_attn, 1)

            def turn_y(j):
                pe.wait_ge(s_y, QT * (j + 1))
                for n in range(2 * QT):
                    src = y[:, n, :] if n < QT else x1[:, QT * j + n - QT, :]
                    ins = nc.tensor.transpose(ps_m[:, n * P:(n + 1) * P], src, ident[:, :])
                ins.then_inc(s_yT, 1)

            def logits(j):
                pe.wait_ge(s_yTact, 2 * (j + 1))
                pe.wait_ge(s_yTlo, j + 1)
                if j == 0:
                    pe.wait_ge(s_wghi, 1)
                    pe.wait_ge(s_wglo, 1)
                for qt in range(QT):
                    t = slice((QT * j + qt) * P, (QT * j + qt + 1) * P)
                    ins = product(ps_m[:, qt * EXPERTS:(qt + 1) * EXPERTS],
                                  (yT_hi[:, t], yT_lo[:, t], wg_hi[:, :], wg_lo[:, :]))
                ins.then_inc(s_logit, 1)

            def turn_comb(h):
                pe.wait_ge(s_comb, h + 1)
                pe.wait_ge(s_expneg, (3, 4)[h])
                for t in range(HTILES):
                    ins = nc.tensor.transpose(ps_m[:, t * P:(t + 1) * P], comb[:, t, :], ident[:, :])
                ins.then_inc(s_combT, 1)

            def up(i):
                h = i // FT
                tok = slice(h * HTOK, (h + 1) * HTOK)
                if i == 0:
                    pe.wait_ge(s_exp, NCH * TILES)
                    pe.wait_ge(s_whi, 2)
                    pe.wait_ge(s_wlo, 2)
                    pe.wait_ge(s_yTlo, QT)
                if i >= 2:
                    pe.wait_ge(s_silu, i - 1)
                product(h1[i % 2], (w_hi[:, 0, w_tile(i)], w_lo[:, 0, w_tile(i)], yT_hi[:, tok], yT_lo[:, tok]))
                if i >= 2:
                    pe.wait_ge(s_gated, i - 1)
                ins = product(h3[i % 2], (w_hi[:, 1, w_tile(i)], w_lo[:, 1, w_tile(i)], yT_hi[:, tok], yT_lo[:, tok]))
                ins.then_inc(s_up, 1)

            def spread_weights(i):
                if is_shared(i):
                    return
                h = i // FT
                pe.wait_ge(s_combT_sb, h + 1)
                if i == 1:
                    pe.wait_ge(s_sel, 1)
                if i < 3:
                    pe.wait_ge(s_pTlo, PAIRS * BATCHES)
                else:
                    pe.wait_ge(s_z, routed_steps(i - 2))
                nc.tensor.matmul(spread[i % 2], sel[:, w_tile(i)], combT[:, h * HTOK:(h + 1) * HTOK],
                                 start=True, stop=True).then_inc(s_spread, 1)

            def down(i):
                h = i // FT
                pe.wait_ge(s_zhi, i + 1)
                if i == 0:
                    pe.wait_ge(s_whi, 3)
                    pe.wait_ge(s_wlo, 3)
                    pe.wait_ge(s_oT, BATCHES)
                if i == FT:
                    pe.wait_ge(s_combT_sb, 2)
                first, last = i % FT == 0, i % FT == FT - 1
                k = i % PT_RING
                nc.tensor.matmul(acc[h][:, :], w_hi[:, 2, w_tile(i)], z_hi[:, k, :], start=first, stop=False)
                nc.tensor.matmul(acc[h][:, :], w_lo[:, 2, w_tile(i)], z_hi[:, k, :], start=False, stop=False)
                pe.wait_ge(s_zlo, i + 1)
                nc.tensor.matmul(acc[h][:, :], w_hi[:, 2, w_tile(i)], z_lo[:, k, :], start=False,
                                 stop=last).then_inc(s_down, 1)

            pe.wait_ge(l_wq, 32)
            nc.tensor.matmul(ps_m[:, 0:D], wq_sb[:, :], wk_sb[:, :], start=True, stop=True).then_inc(s_wqk, 1)
            pe.wait_ge(s_ident, 1)
            turn_x(0)
            pe.wait_ge(s_wqk_sb, 1)
            query(0)
            for b in range(BATCHES + 1):
                for qt in range(QT):
                    before, after = pairs_of(b, qt)
                    if b < BATCHES:
                        score(b, qt, 0)
                    if b >= 3 and qt == 0:
                        logits(b - 3)
                    if b < BATCHES:
                        score(b, qt, 1)
                    if b == 0 and qt == 0:
                        turn_x(1)
                    for g in before:
                        turn(g)
                        if g >= 1:
                            weigh(g - 1)
                    if b < BATCHES:
                        score(b, qt, 2)
                    if b == 0 and qt == 0:
                        query(1)
                    for n, g in enumerate(after):
                        turn(g)
                        weigh(g - 1)
                        if n == 0 and b >= 2:
                            attend(b - 2) if qt == 0 else turn_y(b - 2)
            weigh(PAIRS * BATCHES - 1)
            logits(2)
            for i in range(STEPS + 2):
                if i < STEPS:
                    up(i)
                    spread_weights(i)
                if i >= 2:
                    down(i - 2)
                if i == 0:
                    turn_comb(0)
                if i == 1:
                    attend(3)
                if i == 5:
                    turn_y(3)
                if i == 6:
                    logits(3)
                if i == FT:
                    turn_comb(1)


def kernel(**inputs):
    import numpy as np
    import concourse.bacc as bacc
    from concourse.bass_utils import run_bass_kernel_spmd

    a = {k: np.asarray(v) for k, v in inputs.items()}
    ctx = a["ctx_1024"]
    full = FULL_KT * P
    arrays = {
        "x": a["x"].reshape(TILES, P, D).transpose(1, 0, 2).reshape(P, TILES * D),
        "ctxT": ctx.transpose(0, 2, 1),
        "ctxN": ctx[:, :full].reshape(BATCHES, FULL_KT, P, D).transpose(0, 2, 1, 3).reshape(BATCHES, P, full),
        "ctxTail": ctx[:, full:],
        "wq": a["L0_xattn_Wq"],
        "wk": a["L0_xattn_Wk"],
        "wvT": a["L0_xattn_Wv"].T,
        "wgT": a["L0_ffn_w_gate"].T,
        "w1T": np.concatenate([a["L0_ffn_w1_e"].reshape(-1, D).T, a["L0_ffn_w1_s"].T], axis=1),
        "w3T": np.concatenate([a["L0_ffn_w3_e"].reshape(-1, D).T, a["L0_ffn_w3_s"].T], axis=1),
        "w2T": np.concatenate([a["L0_ffn_w2_e"].transpose(0, 2, 1).reshape(-1, D), a["L0_ffn_w2_s"].T], axis=0)
                 .reshape(FT, P, D).transpose(1, 0, 2).reshape(P, FT * D),
        "g_xattn": a["g_xattn"].reshape(1, 1),
        "g_ffn": a["g_ffn"].reshape(1, 1),
    }
    arrays = {f"in_{k}": np.ascontiguousarray(v) for k, v in arrays.items()}
    nc = bacc.Bacc("TRN2", target_bir_lowering=False, num_devices=1)
    args = [nc.dram_tensor(k, v.shape, mybir.dt.from_np(v.dtype), kind="ExternalInput").ap()
            for k, v in arrays.items()]
    args.append(nc.dram_tensor("out_T", (D, TOKENS), F32, kind="ExternalOutput").ap())
    build(nc, *args)
    r = run_bass_kernel_spmd(nc, [arrays], core_ids=[0])
    return r.results[0]["out_T"].T.reshape(BATCHES, SEQ, D)
```

```python
from contextlib import ExitStack

import concourse.bass as bass
from concourse import mybir

P = 128
D = 128
BATCHES = 4
SEQ = 256
KEYS = 1601
EXPERTS = 16
GROUPS = 4
HIDDEN = 64
EPS = 1e-5

QT = SEQ // P
TILES = BATCHES * QT
TOKENS = BATCHES * SEQ
KT = -(-KEYS // P)
FULL_KT = KEYS // P
TAIL = KEYS - FULL_KT * P
KEYS_EVEN = KEYS + KEYS % 2
PAIRS = -(-KT // 2)
BANK = 512
CHUNKS = ((0, BANK), (BANK, 2 * BANK), (2 * BANK, KEYS))
NCH = len(CHUNKS)
HALVES = 2
HTOK = TOKENS // HALVES
HTILES = TILES // HALVES
FT = EXPERTS * HIDDEN // P + 1
WCOLS = FT * P
STEPS = HALVES * FT
END_STEPS = 2
PT_RING = 3
Z_RING = 3
WARM = 9

ALU = mybir.AluOpType
ACT = mybir.ActivationFunctionType
AX = mybir.AxisListType
F32 = mybir.dt.float32
F32R = mybir.dt.float32r


def build(nc, x, ctxT, ctxN, ctxTail, wq, wk, wvT, wgT, w1T, w3T, w2T, g_xattn, g_ffn, outT):
    with ExitStack() as stack:
        def sb(name, shape, dt=F32):
            return stack.enter_context(nc.sbuf_tensor(name, shape, dt))

        def sem(name):
            return stack.enter_context(nc.semaphore(name))

        ident = sb("ident", [P, P])
        neghalf = sb("neghalf", [P, TILES])
        x_sb = sb("x_sb", [P, TILES, D])
        wq_sb = sb("wq_sb", [P, D])
        wk_sb = sb("wk_sb", [P, D])
        wv_sb = sb("wv_sb", [P, D])
        wqk = sb("wqk", [P, D])
        gates = sb("gates", [P, 2])
        tgates = sb("tgates", [P, 2])
        stats = sb("stats", [P, TILES, 6])
        meanvar = sb("meanvar", [P, TILES, 2])
        vareps = sb("vareps", [P, TILES])
        rstd = sb("rstd", [P, TILES])
        xn = sb("xn", [P, TILES, D])
        xnT = sb("xnT", [P, TOKENS])
        q_hi = sb("q_hi", [P, TOKENS], F32R)
        q_lo = sb("q_lo", [P, TOKENS], F32R)
        cT = sb("cT", [P, 2, KEYS])
        cT_hi = sb("cT_hi", [P, 2, KEYS_EVEN], F32R)
        cT_lo = sb("cT_lo", [P, 2, KEYS_EVEN], F32R)
        cN = sb("cN", [P, BATCHES, KT * D])
        probs = sb("probs", [P, 2, QT, KEYS])
        pT = sb("pT", [P, PT_RING, BANK])
        chunk_max = sb("chunk_max", [P, TILES, NCH])
        neg_max = sb("neg_max", [P, TILES])
        chunk_sum = sb("chunk_sum", [P, TILES, NCH])
        row_sum = sb("row_sum", [P, TILES])
        inv_sum = sb("inv_sum", [P, TILES])
        attn_scale = sb("attn_scale", [P, TILES])
        oT = sb("oT", [P, SEQ])
        x1 = sb("x1", [P, TILES, D])
        stats2 = sb("stats2", [P, TILES, 6])
        meanvar2 = sb("meanvar2", [P, TILES, 2])
        vareps2 = sb("vareps2", [P, TILES])
        rstd2 = sb("rstd2", [P, TILES])
        y = sb("y", [P, QT, D])
        x1T = sb("x1T", [P, TOKENS])
        yT_hi = sb("yT_hi", [P, TOKENS], F32R)
        yT_lo = sb("yT_lo", [P, TOKENS], F32R)
        wg = sb("wg", [P, EXPERTS])
        wg_hi = sb("wg_hi", [P, EXPERTS], F32R)
        wg_lo = sb("wg_lo", [P, EXPERTS], F32R)
        w_raw = sb("w_raw", [P, 2, WCOLS])
        w_hi = sb("w_hi", [P, 3, WCOLS], F32R)
        w_lo = sb("w_lo", [P, 3, WCOLS], F32R)
        logit_sb = sb("logit_sb", [P, TILES, EXPERTS])
        expneg = sb("expneg", [P, HTILES, EXPERTS])
        comb = sb("comb", [P, HTILES, P])
        combT = sb("combT", [P, TOKENS], F32R)
        sel = sb("sel", [P, EXPERTS * HIDDEN], F32R)
        z_hi = sb("z_hi", [P, Z_RING, BANK], F32R)
        z_lo = sb("z_lo", [P, Z_RING, BANK], F32R)
        r_den = sb("r_den", [P, HTILES, EXPERTS])
        r_sig = sb("r_sig", [P, HTILES, EXPERTS])
        r_pair = sb("r_pair", [P, HTILES * GROUPS, 6])
        r_group = sb("r_group", [P, HTILES, GROUPS])
        r_ge = sb("r_ge", [P, HTILES, GROUPS, GROUPS])
        r_gt = sb("r_gt", [P, HTILES, GROUPS, GROUPS])
        r_lower = sb("r_lower", [P, HTILES, GROUPS, GROUPS])
        r_rank = sb("r_rank", [P, HTILES, GROUPS])
        r_off = sb("r_off", [P, HTILES, GROUPS])
        r_masked = sb("r_masked", [P, HTILES, EXPERTS])
        r_top = sb("r_top", [P, HTILES, 8])
        r_above = sb("r_above", [P, HTILES, EXPERTS])
        r_tie = sb("r_tie", [P, HTILES, EXPERTS])
        r_carry = sb("r_carry", [P, HTILES, EXPERTS])
        r_count = sb("r_count", [P, HTILES, EXPERTS])
        r_nabove = sb("r_nabove", [P, HTILES])
        r_w = sb("r_w", [P, HTILES, EXPERTS])
        r_wsum = sb("r_wsum", [P, HTILES])
        r_winv = sb("r_winv", [P, HTILES])

        early = probs[:, 0, :, :].rearrange("p a b -> p (a b)")
        silu = [early[:, k * BANK:(k + 1) * BANK] for k in (0, 1)]
        gated = [early[:, k * BANK:(k + 1) * BANK] for k in (2, 3)]
        z = [early[:, k * BANK:(k + 1) * BANK] for k in (4, 5)]
        out_sb = xnT
        sel_raw = xn[:, :, :].rearrange("p a b -> p (a b)")

        ps_s = stack.enter_context(nc.psum_tensor("ps_s", [P, 4, BANK], F32))
        ps_x = stack.enter_context(nc.psum_tensor("ps_x", [P, 4, BANK], F32))
        ps_t = ps_x[:, 0:2, :]
        ps_o = ps_x[:, 2, :]
        ps_m = ps_x[:, 3, :]
        scores = ps_s[:, :, :].rearrange("p a b -> p (a b)")
        scores_1 = ps_x[:, :, :].rearrange("p a b -> p (a b)")
        h1 = [ps_s[:, 0, :], ps_s[:, 1, :]]
        h3 = [ps_s[:, 2, :], ps_s[:, 3, :]]
        spread = [ps_t[:, 0, :], ps_t[:, 1, :]]
        acc = [ps_o, ps_m]

        l_wq, l_wv, l_wg, l_gate = (sem(n) for n in ("l_wq", "l_wv", "l_wg", "l_gate"))
        l_x = [sem(f"l_x{k}") for k in range(3)]
        l_cT_first = [sem(f"l_cT_first{k}") for k in range(NCH)]
        l_cT = [sem(f"l_cT{k}") for k in range(BATCHES)]
        l_cN = [sem(f"l_cN{k}") for k in range(BATCHES)]
        l_w = [sem(f"l_w{k}") for k in range(3)]
        s_fill = sem("s_fill")
        s_ident = sem("s_ident")
        s_tailz = sem("s_tailz")
        s_consts = sem("s_consts")
        s_sel = sem("s_sel")
        s_tg = sem("s_tg")
        s_wqk = sem("s_wqk")
        s_wqk_sb = sem("s_wqk_sb")
        s_var = sem("s_var")
        s_rstd = sem("s_rstd")
        s_xn = sem("s_xn")
        s_xT = sem("s_xT")
        s_xT_sb = sem("s_xT_sb")
        s_q = sem("s_q")
        s_qhi = sem("s_qhi")
        s_qlo = sem("s_qlo")
        s_cThi = sem("s_cThi")
        s_cTlo0 = sem("s_cTlo0")
        s_cTlo = sem("s_cTlo")
        s_score = sem("s_score")
        s_cmax = sem("s_cmax")
        s_max = sem("s_max")
        s_exp = sem("s_exp")
        s_turn = sem("s_turn")
        s_pT = {"act": sem("s_pT_act"), "dve": sem("s_pT_dve")}
        s_pv = sem("s_pv")
        s_oT = sem("s_oT")
        s_attn = sem("s_attn")
        s_scale = sem("s_scale")
        s_x1 = sem("s_x1")
        s_var2 = sem("s_var2")
        s_rstd2 = sem("s_rstd2")
        s_y = sem("s_y")
        s_yT = sem("s_yT")
        s_yTact = sem("s_yTact")
        s_yTlo = sem("s_yTlo")
        s_st = sem("s_st")
        s_whi = sem("s_whi")
        s_wlo = sem("s_wlo")
        s_wghi = sem("s_wghi")
        s_wglo = sem("s_wglo")
        s_logit = sem("s_logit")
        s_logit_sb = sem("s_logit_sb")
        s_expneg = sem("s_expneg")
        s_route = sem("s_route")
        s_comb = sem("s_comb")
        s_combT = sem("s_combT")
        s_combT_sb = sem("s_combT_sb")
        s_up = sem("s_up")
        s_spread = sem("s_spread")
        s_silu = sem("s_silu")
        s_gated = sem("s_gated")
        s_z = sem("s_z")
        s_zhi = sem("s_zhi")
        s_zlo = sem("s_zlo")
        s_zlo_end = sem("s_zlo_end")
        s_down = sem("s_down")
        s_out = sem("s_out")
        l_out = sem("l_out")

        group_tiles = (range(0, QT), range(QT, 2 * QT), range(2 * QT, TILES))
        NGROUP = len(group_tiles)
        turned_at = (ps_t[:, 0, :], ps_m, ps_m)
        query_at = (ps_t[:, 1, :], ps_m, ps_m)

        def group_cols(k):
            return slice(group_tiles[k][0] * P, (group_tiles[k][-1] + 1) * P)

        def scores_of(s):
            return scores_1 if s == 1 else scores

        def pairs_of(b, qt):
            first = PAIRS * (b - 1)
            if b == 0:
                return [], []
            if qt == 0:
                return [first], [first + 1, first + 2]
            return [first + 3], [first + 4, first + 5, first + 6]

        def pair_tiles(g):
            p = g % PAIRS
            return [t for t in (2 * p, 2 * p + 1) if t < KT]

        def mover(g):
            by_act = [k % PAIRS in (0, 1, 3, 4) for k in range(g + 1)]
            return ("act", sum(by_act)) if by_act[-1] else ("dve", g + 1 - sum(by_act))

        def pair_moved(eng, g):
            who, n = mover(g)
            eng.wait_ge(s_pT[who], n)

        def rows(t):
            return P if t < FULL_KT else TAIL

        def chunk_of(t):
            return min((t * P + rows(t) - 1) // BANK, NCH - 1)

        def is_shared(i):
            return i % FT == 0

        def w_tile(i):
            t = FT - 1 if is_shared(i) else i % FT - 1
            return slice(t * P, (t + 1) * P)

        def routed_steps(i):
            return i + 1 - (i // FT + 1)

        block = stack.enter_context(nc.Block())

        @block.sync
        def _(sp):
            def load_x(k):
                a, e = group_tiles[k][0], group_tiles[k][-1] + 1
                sp.dma_start(x_sb[:, a:e, :], x[:, a * D:e * D]).then_inc(l_x[k], 16)

            load_x(0)
            for c, (a, e) in enumerate(CHUNKS):
                sp.dma_start(cT[:, 0, a:e], ctxT[0][:, a:e]).then_inc(l_cT_first[c], 16)
                if c == 0:
                    load_x(1)
            sp.dma_start(cT[:, 1, :], ctxT[1]).then_inc(l_cT[1], 16)
            load_x(2)
            for b in range(BATCHES):
                if b >= 2:
                    sp.wait_ge(s_cThi, NCH * (b - 1))
                    if b == 2:
                        sp.wait_ge(s_cTlo0, NCH)
                    else:
                        sp.wait_ge(s_cTlo, NCH * (b - 2))
                if b >= 2:
                    sp.dma_start(cT[:, b % 2, :], ctxT[b]).then_inc(l_cT[b], 16)
                sp.dma_start(cN[:, b, 0:FULL_KT * D], ctxN[b]).then_inc(l_cN[b], 16)
                sp.dma_start(cN[0:TAIL, b, FULL_KT * D:KT * D], ctxTail[b]).then_inc(l_cN[b], 16)
                if b == 0:
                    sp.dma_start(gates[:, 0:1], g_xattn.broadcast_to([P, 1])).then_inc(l_gate, 16)
                    sp.dma_start(gates[:, 1:2], g_ffn.broadcast_to([P, 1])).then_inc(l_gate, 16)
                if b == 1:
                    sp.dma_start(wv_sb[:, :], wvT).then_inc(l_wv, 16)
                    sp.dma_start(wg[:, :], wgT).then_inc(l_wg, 16)
                    for k, w in enumerate((w1T, w3T)):
                        sp.dma_start(w_raw[:, k, :], w).then_inc(l_w[k], 16)
            sp.wait_ge(s_wlo, 1)
            sp.dma_start(w_raw[:, 0, :], w2T).then_inc(l_w[2], 16)
            for n in range(2 * HALVES):
                sp.wait_ge(s_out, n + 1)
                w = HTOK // 2
                sp.dma_start(outT[:, n * w:(n + 1) * w], out_sb[:, n * w:(n + 1) * w]).then_inc(l_out, 16)
            sp.wait_ge(l_out, 16 * 2 * HALVES)

        @block.gpsimd
        def _(pool):
            nc.gpsimd.memset(ident[:, :], 1.0).then_inc(s_fill, 1)
            nc.gpsimd.memset(neghalf[:, :], -0.5).then_inc(s_fill, 1)
            pool.wait_ge(s_fill, 2)
            nc.gpsimd.affine_select(out=ident[:, :], in_=ident[:, :], compare_op=ALU.is_equal, fill=0.0,
                                    base=0, pattern=[[-1, P]], channel_multiplier=1).then_inc(s_ident, 1)

            def rsqrt(var, out, tiles, ready, n, done):
                pool.wait_ge(ready, n)
                a, b = tiles[0], tiles[-1] + 1
                nc.gpsimd.tensor_tensor(out[:, a:b], var[:, a:b], neghalf[:, a:b], ALU.pow).then_inc(done, 1)

            rsqrt(vareps, rstd, group_tiles[0], s_var, 1, s_rstd)
            rsqrt(vareps, rstd, group_tiles[1], s_var, 2, s_rstd)

            def cT_low(b):
                for c, (a, e) in enumerate(CHUNKS):
                    pool.wait_ge(s_cThi, NCH * b + c + 1)
                    if b >= 2:
                        pool.wait_ge(s_score, NCH * QT * (b - 1))
                    nc.gpsimd.tensor_tensor(cT_lo[:, b % 2, a:e], cT[:, b % 2, a:e],
                                            cT_hi[:, b % 2, a:e].bitcast(F32), ALU.subtract).then_inc(s_cTlo, 1)

            def w_low(k):
                pool.wait_ge(s_whi, k + 1)
                nc.gpsimd.tensor_tensor(w_lo[:, k, :], w_raw[:, k % 2, :], w_hi[:, k, :].bitcast(F32),
                                        ALU.subtract).then_inc(s_wlo, 1)

            def batch_rsqrt2(j):
                rsqrt(vareps2, rstd2, range(QT * j, QT * j + QT), s_var2, j + 1, s_rstd2)

            cT_low(1)
            rsqrt(vareps, rstd, group_tiles[2], s_var, 3, s_rstd)
            cT_low(2)
            sel3 = sel_raw.rearrange("p (e f) -> p e f", f=HIDDEN)
            pool.wait_ge(s_xT, NGROUP)
            nc.gpsimd.memset(sel_raw, 0.0).then_inc(s_fill, 1)
            pool.wait_ge(s_fill, 3)
            nc.gpsimd.affine_select(out=sel3, in_=sel3, compare_op=ALU.not_equal, fill=1.0, base=0,
                                    pattern=[[-1, EXPERTS], [0, HIDDEN]], channel_multiplier=1).then_inc(s_fill, 1)
            pool.wait_ge(s_fill, 4)
            nc.gpsimd.affine_select(out=sel3, in_=sel3, compare_op=ALU.not_equal, fill=1.0, base=-EXPERTS,
                                    pattern=[[-1, EXPERTS], [0, HIDDEN]], channel_multiplier=1).then_inc(s_fill, 1)
            w_low(0)
            cT_low(3)
            batch_rsqrt2(0)
            w_low(1)
            batch_rsqrt2(1)
            w_low(2)
            batch_rsqrt2(2)
            for i in range(STEPS - END_STEPS):
                pool.wait_ge(s_zhi, i + 1)
                if i >= Z_RING:
                    pool.wait_ge(s_down, i - Z_RING + 1)
                nc.gpsimd.tensor_tensor(z_lo[:, i % Z_RING, :], z[i % 2], z_hi[:, i % Z_RING, :].bitcast(F32),
                                        ALU.subtract).then_inc(s_zlo, 1)
                if i == 0:
                    batch_rsqrt2(3)

        @block.scalar
        def _(act):
            act.dma_start(wq_sb[:, :], wq).then_inc(l_wq, 16)
            act.dma_start(wk_sb[:, :], wk).then_inc(l_wq, 16)

            def cT_high(b, c):
                a, e = CHUNKS[c]
                act.wait_ge(l_cT_first[c] if b == 0 else l_cT[b], 16)
                if b >= 2:
                    act.wait_ge(s_score, NCH * QT * (b - 1))
                nc.scalar.copy(cT_hi[:, b % 2, a:e], cT[:, b % 2, a:e]).then_inc(s_cThi, 1)

            def move_x(k):
                act.wait_ge(s_xT, k + 1)
                cols = group_cols(k)
                nc.scalar.copy(xnT[:, cols], turned_at[k][:, 0:cols.stop - cols.start]).then_inc(s_xT_sb, 1)

            def q_high(k):
                act.wait_ge(s_q, k + 1)
                cols = group_cols(k)
                nc.scalar.copy(q_hi[:, cols], query_at[k][:, 0:cols.stop - cols.start]).then_inc(s_qhi, 1)

            def exponential(b, qt, c):
                s = QT * b + qt
                a, e = CHUNKS[c]
                act.wait_ge(s_max, s + 1)
                if b >= 2:
                    act.wait_ge(s_turn, PAIRS * (b - 1))
                nc.scalar.activation(probs[:, b % 2, qt, a:e], scores_of(s)[:, a:e], ACT.Exp, bias=neg_max[:, s:s + 1],
                                     accum_out=chunk_sum[:, s, c:c + 1]).then_inc(s_exp, 1)

            def move_pair(g):
                if mover(g)[0] != "act":
                    return
                w = len(pair_tiles(g)) * SEQ
                r = rows(pair_tiles(g)[-1])
                act.wait_ge(s_turn, g + 1)
                if g >= PT_RING:
                    act.wait_ge(s_pv, g - PT_RING + 1)
                nc.scalar.copy(pT[0:r, g % PT_RING, 0:w], ps_t[0:r, g % 2, 0:w]).then_inc(s_pT["act"], 1)

            def move_o(j):
                act.wait_ge(s_pv, PAIRS * (j + 1))
                if j >= 1:
                    act.wait_ge(s_attn, j)
                nc.scalar.copy(oT[:, :], ps_o[:, 0:SEQ]).then_inc(s_oT, 1)

            def move_y(j):
                a = SEQ * j
                act.wait_ge(s_yT, j + 1)
                nc.scalar.copy(yT_hi[:, a:a + SEQ], ps_m[:, 0:SEQ]).then_inc(s_yTact, 1)
                nc.scalar.copy(x1T[:, a:a + SEQ], ps_m[:, SEQ:2 * SEQ]).then_inc(s_yTact, 1)

            def move_logits(j):
                act.wait_ge(s_logit, j + 1)
                nc.scalar.copy(logit_sb[:, QT * j:QT * j + QT, :].rearrange("p a b -> p (a b)"),
                               ps_m[:, 0:QT * EXPERTS]).then_inc(s_logit_sb, 1)

            def exp_logits(h):
                act.wait_ge(s_logit_sb, QT * (h + 1))
                if h >= 1:
                    act.wait_ge(s_comb, h)
                nc.scalar.activation(expneg[:], logit_sb[:, HTILES * h:HTILES * (h + 1), :], ACT.Exp,
                                     scale=-1.0).then_inc(s_expneg, 1)

            cT_high(0, 0)
            move_x(0)
            act.wait_ge(s_wqk, 1)
            nc.scalar.copy(wqk[:, :], ps_m[:, 0:D]).then_inc(s_wqk_sb, 1)
            q_high(0)
            cT_high(0, 1)
            cT_high(0, 2)
            move_x(1)
            q_high(1)
            for c in range(NCH):
                cT_high(1, c)

            def silu_of(i):
                act.wait_ge(s_up, i + 1)
                if i == 0:
                    act.wait_ge(s_turn, PAIRS * (BATCHES - 1))
                if i >= 2:
                    act.wait_ge(s_gated, i - 1)
                nc.scalar.activation(silu[i % 2], h1[i % 2], ACT.Silu).then_inc(s_silu, 1)

            def z_high(i):
                if is_shared(i):
                    act.wait_ge(s_gated, i + 1)
                else:
                    act.wait_ge(s_z, routed_steps(i))
                if i >= Z_RING:
                    act.wait_ge(s_down, i - Z_RING + 1)
                nc.scalar.copy(z_hi[:, i % Z_RING, :], z[i % 2]).then_inc(s_zhi, 1)

            def move_comb(h):
                act.wait_ge(s_combT, h + 1)
                nc.scalar.copy(combT[:, h * HTOK:(h + 1) * HTOK], ps_m[:, :]).then_inc(s_combT_sb, 1)

            for b in range(BATCHES):
                for qt in range(QT):
                    before, after = pairs_of(b, qt)
                    if b == 3 and qt == 0:
                        move_logits(0)
                    if b == 1 and qt == 0:
                        act.wait_ge(l_gate, 32)
                        nc.scalar.activation(tgates[:, :], gates[:, :], ACT.Tanh).then_inc(s_tg, 1)
                    if b == 1 and qt == 1:
                        move_x(2)
                    for g in before:
                        move_pair(g)
                    if b == 1 and qt == 1:
                        q_high(2)
                    for g in after[:1]:
                        move_pair(g)
                    if b >= 2 and qt == 0:
                        move_o(b - 2)
                    for c in range(NCH):
                        exponential(b, qt, c)
                        if 1 + c < len(after):
                            move_pair(after[1 + c])
                        if qt == 0 and 1 <= b < BATCHES - 1:
                            cT_high(b + 1, c)
                    if b >= 2 and qt == 1:
                        move_y(b - 2)
            first = PAIRS * (BATCHES - 1)
            move_logits(1)
            exp_logits(0)
            move_pair(first)
            silu_of(0)
            move_pair(first + 1)
            move_o(2)
            move_pair(first + 2)
            move_pair(first + 3)
            silu_of(1)
            move_pair(first + 4)
            move_pair(first + 5)
            move_y(2)
            move_pair(first + 6)
            move_o(3)
            z_high(0)
            move_logits(2)
            move_comb(0)
            for i in range(2, STEPS + 1):
                if i < STEPS:
                    silu_of(i)
                z_high(i - 1)
                if i == 5:
                    move_y(3)
                if i == 6:
                    move_logits(3)
                    exp_logits(1)
                if i == FT + 1:
                    move_comb(1)

        @block.vector
        def _(dve):
            steps = [0]

            def link(ins):
                steps[0] += 1
                ins.then_inc(s_st, 1)
                dve.wait_ge(s_st, steps[0])

            routed = [0]

            def route(ins):
                routed[0] += 1
                ins.then_inc(s_route, 1)
                dve.wait_ge(s_route, routed[0])

            def norm_stats(src, st, mv, var, tiles, done):
                for t in tiles:
                    ins = nc.vector.bn_stats(st[:, t, :], src[:, t, :])
                link(ins)
                for t in tiles:
                    ins = nc.vector.bn_aggr(mv[:, t, :], st[:, t, :])
                link(ins)
                a, b = tiles[0], tiles[-1] + 1
                nc.vector.tensor_scalar(var[:, a:b], mv[:, a:b, 1], EPS, None, ALU.add).then_inc(done, 1)

            def x_stats(k):
                dve.wait_ge(l_x[k], 16)
                norm_stats(x_sb, stats, meanvar, vareps, group_tiles[k], s_var)

            def norm_x(k):
                dve.wait_ge(s_rstd, k + 1)
                for t in group_tiles[k]:
                    ins = nc.vector.tensor_scalar(xn[:, t, :], x_sb[:, t, :], meanvar[:, t, 0:1], rstd[:, t:t + 1],
                                                  ALU.subtract, ALU.mult)
                    ins.then_inc(s_xn, 1)

            def q_low(k):
                dve.wait_ge(s_qhi, k + 1)
                cols = group_cols(k)
                nc.vector.tensor_tensor(q_lo[:, cols], query_at[k][:, 0:cols.stop - cols.start],
                                        q_hi[:, cols].bitcast(F32), ALU.subtract).then_inc(s_qlo, 1)

            def cT_low0(c):
                a, e = CHUNKS[c]
                dve.wait_ge(s_cThi, c + 1)
                nc.vector.tensor_tensor(cT_lo[:, 0, a:e], cT[:, 0, a:e], cT_hi[:, 0, a:e].bitcast(F32),
                                        ALU.subtract).then_inc(s_cTlo0, 1)

            def w_high(k):
                dve.wait_ge(l_w[k], 16)
                nc.vector.tensor_copy(w_hi[:, k, :], w_raw[:, k % 2, :]).then_inc(s_whi, 1)

            def chunk_maximum(b, qt, c):
                s = QT * b + qt
                a, e = CHUNKS[c]
                dve.wait_ge(s_score, NCH * s + c + 1)
                nc.vector.tensor_reduce(chunk_max[:, s, c:c + 1], scores_of(s)[:, a:e], AX.X, ALU.max).then_inc(s_cmax, 1)

            def maximum(b, qt):
                s = QT * b + qt
                dve.wait_ge(s_cmax, NCH * (s + 1))
                nc.vector.tensor_reduce(neg_max[:, s:s + 1], chunk_max[:, s, :], AX.X, ALU.max,
                                        negate=True).then_inc(s_max, 1)

            def move_pair(g):
                if mover(g)[0] != "dve":
                    return
                w = len(pair_tiles(g)) * SEQ
                r = rows(pair_tiles(g)[-1])
                dve.wait_ge(s_turn, g + 1)
                if g >= PT_RING:
                    dve.wait_ge(s_pv, g - PT_RING + 1)
                nc.vector.tensor_copy(pT[0:r, g % PT_RING, 0:w], ps_t[0:r, g % 2, 0:w]).then_inc(s_pT["dve"], 1)

            def residual(j):
                a, e = QT * j, QT * j + QT
                dve.wait_ge(s_exp, NCH * e)
                link(nc.vector.tensor_reduce(row_sum[:, a:e], chunk_sum[:, a:e, :], AX.X, ALU.add))
                link(nc.vector.reciprocal(inv_sum[:, a:e], row_sum[:, a:e]))
                dve.wait_ge(s_tg, 1)
                link(nc.vector.tensor_scalar(attn_scale[:, a:e], inv_sum[:, a:e], tgates[:, 0:1], None, ALU.mult))
                dve.wait_ge(s_attn, j + 1)
                for t in range(a, e):
                    ins = nc.vector.scalar_tensor_tensor(out=x1[:, t, :], in0=ps_m[:, (t - a) * D:(t - a + 1) * D],
                                                         scalar=attn_scale[:, t:t + 1], in1=x_sb[:, t, :],
                                                         op0=ALU.mult, op1=ALU.add)
                    ins.then_inc(s_x1, 1)
                dve.wait_ge(s_x1, e)
                norm_stats(x1, stats2, meanvar2, vareps2, range(a, e), s_var2)

            def norm_y(j):
                a = QT * j
                dve.wait_ge(s_rstd2, j + 1)
                if j >= 1:
                    dve.wait_ge(s_yT, j)
                for t in range(a, a + QT):
                    nc.vector.tensor_scalar(y[:, t - a, :], x1[:, t, :], meanvar2[:, t, 0:1], rstd2[:, t:t + 1],
                                            ALU.subtract, ALU.mult).then_inc(s_y, 1)

            def yT_low(j):
                a = SEQ * j
                dve.wait_ge(s_yTact, 2 * (j + 1))
                nc.vector.tensor_tensor(yT_lo[:, a:a + SEQ], ps_m[:, 0:SEQ], yT_hi[:, a:a + SEQ].bitcast(F32),
                                        ALU.subtract).then_inc(s_yTlo, 1)

            def bc(v, n):
                return v.unsqueeze(len(v.shape)).broadcast_to(list(v.shape) + [n])

            def router_constants():
                nc.vector.memset(comb[:], 0.0)
                nc.vector.memset(r_lower[:], 0.0)
                link(nc.vector.memset(r_carry[:], 1.0))
                nc.vector.memset(r_carry[:, :, 0:1], 0.0)
                for g in range(1, GROUPS):
                    ins = nc.vector.memset(r_lower[:, :, g, 0:g], 1.0)
                ins.then_inc(s_consts, 1)

            def router(h, part):
                if part == 0:
                    dve.wait_ge(s_expneg, h + 1)
                    route(nc.vector.tensor_scalar(r_den[:], expneg[:], 1.0, None, ALU.add))
                    route(nc.vector.reciprocal(r_sig[:], r_den[:]))
                    sg = r_sig[:].rearrange("p t (g m) -> p (t g) m", g=GROUPS)
                    nc.vector.tensor_tensor(r_pair[:, :, 0:2], sg[:, :, 0:2], sg[:, :, 2:4], ALU.add)
                    nc.vector.tensor_tensor(r_pair[:, :, 2:4], sg[:, :, 0:4:2], sg[:, :, 1:4:2], ALU.add)
                    nc.vector.tensor_tensor(r_pair[:, :, 4:5], sg[:, :, 0:1], sg[:, :, 3:4], ALU.add)
                    route(nc.vector.tensor_tensor(r_pair[:, :, 5:6], sg[:, :, 1:2], sg[:, :, 2:3], ALU.add))
                    route(nc.vector.tensor_reduce(r_group[:].rearrange("p t g -> p (t g)"), r_pair[:], AX.X, ALU.max))
                if part == 1:
                    dve.wait_ge(s_consts, 1)
                    mine = r_group[:].unsqueeze(3).broadcast_to([P, HTILES, GROUPS, GROUPS])
                    other = r_group[:].unsqueeze(2).broadcast_to([P, HTILES, GROUPS, GROUPS])
                    nc.vector.tensor_tensor(r_gt[:], other, mine, ALU.is_gt)
                    route(nc.vector.tensor_tensor(r_ge[:], other, mine, ALU.is_ge))
                    route(nc.vector.tensor_tensor(r_ge[:], r_ge[:], r_lower[:], ALU.mult))
                    route(nc.vector.tensor_tensor(r_gt[:], r_gt[:], r_ge[:], ALU.max))
                    route(nc.vector.tensor_reduce(r_rank[:], r_gt[:], AX.X, ALU.add))
                    route(nc.vector.tensor_scalar(r_off[:], r_rank[:], 1.5, -4.0, ALU.is_gt, ALU.mult))
                    n = EXPERTS // GROUPS
                    sg = r_sig[:].rearrange("p t (g m) -> p (t g) m", g=GROUPS)
                    mk = r_masked[:].rearrange("p t (g m) -> p (t g) m", g=GROUPS)
                    route(nc.vector.tensor_tensor(mk, sg, bc(r_off[:].rearrange("p t g -> p (t g)"), n), ALU.add))
                if part == 2:
                    for t in range(HTILES):
                        ins = nc.vector.max(r_top[:, t, :], r_masked[:, t, :])
                    route(ins)
                    fourth = r_top[:, :, 3:4].broadcast_to([P, HTILES, EXPERTS])
                    nc.vector.tensor_tensor(r_above[:], r_masked[:], fourth, ALU.is_gt)
                    route(nc.vector.tensor_tensor(r_tie[:], r_masked[:], fourth, ALU.is_equal))
                    nc.vector.tensor_reduce(r_nabove[:], r_above[:], AX.X, ALU.add)
                    route(nc.vector.tensor_tensor_scan(r_count[:].rearrange("p t e -> p (t e)"),
                                                       r_carry[:].rearrange("p t e -> p (t e)"),
                                                       r_tie[:].rearrange("p t e -> p (t e)"), 0.0,
                                                       ALU.mult, ALU.add))
                    route(nc.vector.tensor_tensor(r_count[:], r_count[:], bc(r_nabove[:], EXPERTS), ALU.add))
                    route(nc.vector.scalar_tensor_tensor(out=r_tie[:].rearrange("p t e -> p (t e)"),
                                                         in0=r_count[:].rearrange("p t e -> p (t e)"), scalar=4.5,
                                                         in1=r_tie[:].rearrange("p t e -> p (t e)"),
                                                         op0=ALU.is_lt, op1=ALU.mult))
                    route(nc.vector.tensor_tensor(r_above[:], r_above[:], r_tie[:], ALU.add))
                if part == 3:
                    route(nc.vector.tensor_tensor(r_w[:], r_above[:], r_sig[:], ALU.mult))
                    route(nc.vector.tensor_reduce(r_wsum[:], r_w[:], AX.X, ALU.add))
                    route(nc.vector.tensor_scalar(r_wsum[:], r_wsum[:], 1e-6, None, ALU.add))
                    route(nc.vector.reciprocal(r_winv[:], r_wsum[:]))
                    route(nc.vector.tensor_tensor(r_w[:], r_w[:], bc(r_winv[:], EXPERTS), ALU.mult))
                    if h >= 1:
                        dve.wait_ge(s_combT, h)
                    route(nc.vector.tensor_copy(comb[:, :, 0:EXPERTS].bitcast(F32R), r_w[:]))
                    nc.vector.tensor_tensor(comb[:, :, EXPERTS:2 * EXPERTS], r_w[:], comb[:, :, 0:EXPERTS],
                                            ALU.subtract).then_inc(s_comb, 1)

            nc.vector.memset(cT_hi[:, :, KEYS:KEYS_EVEN].bitcast(F32), 0.0).then_inc(s_tailz, 1)
            nc.vector.memset(cT_lo[:, :, KEYS:KEYS_EVEN].bitcast(F32), 0.0).then_inc(s_tailz, 1)
            router_constants()
            x_stats(0)
            norm_x(0)
            x_stats(1)
            cT_low0(0)
            norm_x(1)
            q_low(0)
            cT_low0(1)
            cT_low0(2)

            def gate(i):
                dve.wait_ge(s_silu, i + 1)
                if i >= 2:
                    dve.wait_ge(s_zhi, i - 1)
                    dve.wait_ge(s_zlo, min(i - 1, STEPS - END_STEPS))
                to = z if is_shared(i) else gated
                nc.vector.tensor_tensor(to[i % 2], silu[i % 2], h3[i % 2], ALU.mult).then_inc(s_gated, 1)
                if not is_shared(i):
                    dve.wait_ge(s_gated, i + 1)
                    dve.wait_ge(s_spread, routed_steps(i))
                    nc.vector.tensor_tensor(z[i % 2], gated[i % 2], spread[i % 2], ALU.mult).then_inc(s_z, 1)

            def finish(h):
                dve.wait_ge(s_down, FT * (h + 1))
                w = HTOK // 2
                for n in range(2):
                    a = h * HTOK + n * w
                    nc.vector.scalar_tensor_tensor(out=out_sb[:, a:a + w], in0=acc[h][:, n * w:(n + 1) * w],
                                                   scalar=tgates[:, 1:2], in1=x1T[:, a:a + w],
                                                   op0=ALU.mult, op1=ALU.add).then_inc(s_out, 1)

            def z_low(i):
                dve.wait_ge(s_zhi, i + 1)
                dve.wait_ge(s_down, i - Z_RING + 1)
                nc.vector.tensor_tensor(z_lo[:, i % Z_RING, :], z[i % 2], z_hi[:, i % Z_RING, :].bitcast(F32),
                                        ALU.subtract).then_inc(s_zlo_end, 1)

            for b in range(BATCHES):
                for qt in range(QT):
                    before, after = pairs_of(b, qt)
                    chunk_maximum(b, qt, 0)
                    if b == 0 and qt == 0:
                        q_low(1)
                    chunk_maximum(b, qt, 1)
                    for g in before:
                        move_pair(g)
                    if b >= 2 and qt == 1:
                        norm_y(b - 2)
                    chunk_maximum(b, qt, 2)
                    maximum(b, qt)
                    if b == 0 and qt == 1:
                        x_stats(2)
                    if b == 1 and qt == 0:
                        norm_x(2)
                    if b == 1 and qt == 1:
                        q_low(2)
                    for n, g in enumerate(after):
                        move_pair(g)
                        if n == 1 and b >= 2 and qt == 0:
                            residual(b - 2)
                    if b >= 2 and qt == 1:
                        yT_low(b - 2)
                    if qt == 1 and b < 3:
                        w_high(b)
                    if b == 2 and qt == 0:
                        dve.wait_ge(l_wg, 16)
                        nc.vector.tensor_copy(wg_hi[:, :], wg[:, :]).then_inc(s_wghi, 1)
                        dve.wait_ge(s_wghi, 1)
                        nc.vector.tensor_tensor(wg_lo[:, :], wg[:, :], wg_hi[:, :].bitcast(F32),
                                                ALU.subtract).then_inc(s_wglo, 1)
                    if b == 3 and qt == 0:
                        dve.wait_ge(s_fill, 5)
                        nc.vector.tensor_copy(sel[:, :], sel_raw).then_inc(s_sel, 1)
            first = PAIRS * (BATCHES - 1)
            move_pair(first)
            router(0, 0)
            move_pair(first + 1)
            gate(0)
            move_pair(first + 2)
            residual(2)
            move_pair(first + 3)
            router(0, 1)
            move_pair(first + 4)
            norm_y(2)
            move_pair(first + 5)
            router(0, 2)
            move_pair(first + 6)
            yT_low(2)
            router(0, 3)
            for i in range(1, STEPS):
                gate(i)
                if i == 1:
                    residual(3)
                if i == 3:
                    norm_y(3)
                if i == 4:
                    yT_low(3)
                if 6 <= i < 10:
                    router(1, i - 6)
                if i == FT + 2:
                    finish(0)
                if i >= STEPS - END_STEPS:
                    z_low(i)
            finish(1)

        @block.tensor
        def _(pe):
            def product(out, parts):
                lh, ll, rh, rl = parts
                nc.tensor.matmul(out, lh, rh, start=True, stop=False)
                nc.tensor.matmul(out, lh, rl, start=False, stop=False)
                return nc.tensor.matmul(out, ll, rh, start=False, stop=True)

            def turn_x(k):
                if k == 1:
                    pe.wait_ge(s_wqk_sb, 1)
                if k == 2:
                    pe.wait_ge(s_exp, NCH * QT)
                for n, t in enumerate(group_tiles[k]):
                    pe.wait_ge(s_xn, t + 1)
                    ins = nc.tensor.transpose(turned_at[k][:, n * P:(n + 1) * P], xn[:, t, :], ident[:, :])
                ins.then_inc(s_xT, 1)

            def query(k):
                pe.wait_ge(s_xT_sb, k + 1)
                cols = group_cols(k)
                nc.tensor.matmul(query_at[k][:, 0:cols.stop - cols.start], wqk[:, :], xnT[:, cols],
                                 start=True, stop=True).then_inc(s_q, 1)

            def score(b, qt, c):
                s = QT * b + qt
                a, e = CHUNKS[c]
                if s == 1 and c == NCH - 1:
                    pe.wait_ge(s_qlo, 2)
                if s >= 2:
                    last = 0 if s == 2 else s - 1
                    pe.wait_ge(s_exp, NCH * last + c + 1)
                if c == 0 and qt == 0 and b < NGROUP:
                    pe.wait_ge(s_qhi, b + 1)
                    pe.wait_ge(s_qlo, b + 1)
                pe.wait_ge(s_cThi, NCH * b + c + 1)
                if b == 0:
                    pe.wait_ge(s_cTlo0, c + 1)
                else:
                    pe.wait_ge(s_cTlo, NCH * (b - 1) + c + 1)
                q = slice(s * P, (s + 1) * P)
                if s == 0 and c == 0:
                    pe.wait_ge(s_tailz, 2)
                for k in range(a, e, BANK):
                    m = slice(k, min(k + BANK, KEYS_EVEN))
                    ins = product(scores_of(s)[:, m], (q_hi[:, q], q_lo[:, q], cT_hi[:, b % 2, m], cT_lo[:, b % 2, m]))
                ins.then_inc(s_score, 1)

            def turn(g):
                b = g // PAIRS
                if g < 2:
                    pe.wait_ge(s_exp, NCH + g + 1)
                else:
                    pair_moved(pe, g - 2)
                for n, t in enumerate(pair_tiles(g)):
                    pe.wait_ge(s_exp, NCH * (QT * b + 1) + chunk_of(t) + 1)
                    for qt in range(QT):
                        o = (n * QT + qt) * P
                        ins = nc.tensor.transpose(ps_t[0:rows(t), g % 2, o:o + P],
                                                  probs[:, b % 2, qt, t * P:t * P + rows(t)], ident[:, :])
                ins.then_inc(s_turn, 1)

            def weigh(g):
                b = g // PAIRS
                if g % PAIRS == 0:
                    pe.wait_ge(l_cN[b], 32)
                    if b == 0:
                        pe.wait_ge(s_exp, NCH * QT)
                    else:
                        pe.wait_ge(s_oT, b)
                pair_moved(pe, g)
                for n, t in enumerate(pair_tiles(g)):
                    r = rows(t)
                    ins = nc.tensor.matmul(ps_o[:, 0:SEQ], cN[0:r, b, t * D:(t + 1) * D],
                                           pT[0:r, g % PT_RING, n * SEQ:(n + 1) * SEQ],
                                           start=(t == 0), stop=(t == KT - 1))
                ins.then_inc(s_pv, 1)

            def attend(j):
                pe.wait_ge(s_oT, j + 1)
                if j == 0:
                    pe.wait_ge(l_wv, 16)
                    pe.wait_ge(s_qlo, NGROUP)
                elif j < BATCHES - 1:
                    pe.wait_ge(s_logit_sb, j)
                else:
                    pe.wait_ge(s_combT_sb, 1)
                for qt in range(QT):
                    ins = nc.tensor.matmul(ps_m[:, qt * D:(qt + 1) * D], oT[:, qt * P:(qt + 1) * P], wv_sb[:, :],
                                           start=True, stop=True)
                ins.then_inc(s_attn, 1)

            def turn_y(j):
                pe.wait_ge(s_y, QT * (j + 1))
                for n in range(2 * QT):
                    src = y[:, n, :] if n < QT else x1[:, QT * j + n - QT, :]
                    ins = nc.tensor.transpose(ps_m[:, n * P:(n + 1) * P], src, ident[:, :])
                ins.then_inc(s_yT, 1)

            def logits(j):
                pe.wait_ge(s_yTact, 2 * (j + 1))
                pe.wait_ge(s_yTlo, j + 1)
                if j == 0:
                    pe.wait_ge(s_wghi, 1)
                    pe.wait_ge(s_wglo, 1)
                for qt in range(QT):
                    t = slice((QT * j + qt) * P, (QT * j + qt + 1) * P)
                    ins = product(ps_m[:, qt * EXPERTS:(qt + 1) * EXPERTS],
                                  (yT_hi[:, t], yT_lo[:, t], wg_hi[:, :], wg_lo[:, :]))
                ins.then_inc(s_logit, 1)

            def turn_comb(h):
                pe.wait_ge(s_comb, h + 1)
                pe.wait_ge(s_logit_sb, (3, 4)[h])
                for t in range(HTILES):
                    ins = nc.tensor.transpose(ps_m[:, t * P:(t + 1) * P], comb[:, t, :], ident[:, :])
                ins.then_inc(s_combT, 1)

            def up(i):
                h = i // FT
                tok = slice(h * HTOK, (h + 1) * HTOK)
                if i == 0:
                    pe.wait_ge(s_exp, NCH * TILES)
                    pe.wait_ge(s_whi, 2)
                    pe.wait_ge(s_wlo, 2)
                    pe.wait_ge(s_yTlo, QT)
                if i >= 2:
                    pe.wait_ge(s_silu, i - 1)
                product(h1[i % 2], (w_hi[:, 0, w_tile(i)], w_lo[:, 0, w_tile(i)], yT_hi[:, tok], yT_lo[:, tok]))
                if i >= 2:
                    pe.wait_ge(s_gated, i - 1)
                ins = product(h3[i % 2], (w_hi[:, 1, w_tile(i)], w_lo[:, 1, w_tile(i)], yT_hi[:, tok], yT_lo[:, tok]))
                ins.then_inc(s_up, 1)

            def spread_weights(i):
                if is_shared(i):
                    return
                h = i // FT
                pe.wait_ge(s_combT_sb, h + 1)
                if i == 1:
                    pe.wait_ge(s_sel, 1)
                if i < 3:
                    pair_moved(pe, PAIRS * BATCHES - i)
                else:
                    pe.wait_ge(s_z, routed_steps(i - 2))
                nc.tensor.matmul(spread[i % 2], sel[:, w_tile(i)], combT[:, h * HTOK:(h + 1) * HTOK],
                                 start=True, stop=True).then_inc(s_spread, 1)

            def down(i):
                h = i // FT
                pe.wait_ge(s_zhi, i + 1)
                if i == 0:
                    pe.wait_ge(s_whi, 3)
                    pe.wait_ge(s_wlo, 3)
                    pe.wait_ge(s_oT, BATCHES)
                if i == FT:
                    pe.wait_ge(s_combT_sb, 2)
                first, last = i % FT == 0, i % FT == FT - 1
                k = i % Z_RING
                nc.tensor.matmul(acc[h][:, :], w_hi[:, 2, w_tile(i)], z_hi[:, k, :], start=first, stop=False)
                nc.tensor.matmul(acc[h][:, :], w_lo[:, 2, w_tile(i)], z_hi[:, k, :], start=False, stop=False)
                if i < STEPS - END_STEPS:
                    pe.wait_ge(s_zlo, i + 1)
                else:
                    pe.wait_ge(s_zlo_end, i - (STEPS - END_STEPS) + 1)
                nc.tensor.matmul(acc[h][:, :], w_hi[:, 2, w_tile(i)], z_lo[:, k, :], start=False,
                                 stop=last).then_inc(s_down, 1)

            def unit(g):
                turn(g)
                if g >= 2:
                    weigh(g - 2)

            pe.wait_ge(s_ident, 1)
            for _ in range(WARM):
                nc.tensor.matmul(scores[:, 0:P], ident[:, :], ident[:, :], start=True, stop=True)
            turn_x(0)
            pe.wait_ge(l_wq, 32)
            nc.tensor.matmul(ps_m[:, 0:D], wq_sb[:, :], wk_sb[:, :], start=True, stop=True).then_inc(s_wqk, 1)
            pe.wait_ge(s_wqk_sb, 1)
            query(0)
            turn_x(1)
            for b in range(BATCHES):
                for qt in range(QT):
                    before, after = pairs_of(b, qt)
                    score(b, qt, 0)
                    if b == 3 and qt == 0:
                        logits(0)
                    if b == 0 and qt == 0:
                        query(1)
                    score(b, qt, 1)
                    if b == 1 and qt == 1:
                        turn_x(2)
                    for g in before:
                        unit(g)
                    if b == 1 and qt == 1:
                        query(2)
                    score(b, qt, 2)
                    for n, g in enumerate(after):
                        unit(g)
                        if n == 1 and b >= 2:
                            attend(b - 2) if qt == 0 else turn_y(b - 2)
            first = PAIRS * (BATCHES - 1)
            logits(1)
            unit(first)
            up(0)
            unit(first + 1)
            unit(first + 2)
            attend(2)
            unit(first + 3)
            up(1)
            unit(first + 4)
            unit(first + 5)
            turn_y(2)
            unit(first + 6)
            weigh(first + 5)
            weigh(first + 6)
            logits(2)
            turn_comb(0)
            spread_weights(1)
            for i in range(2, STEPS + 2):
                if i < STEPS:
                    up(i)
                if i == 2:
                    attend(3)
                if i < STEPS and i != FT + 1:
                    spread_weights(i)
                down(i - 2)
                if i == 4:
                    turn_y(3)
                if i == 5:
                    logits(3)
                if i == FT + 1:
                    turn_comb(1)
                    spread_weights(i)


def kernel(**inputs):
    import numpy as np
    import concourse.bacc as bacc
    from concourse.bass_utils import run_bass_kernel_spmd

    a = {k: np.asarray(v) for k, v in inputs.items()}
    ctx = a["ctx_1024"]
    full = FULL_KT * P
    arrays = {
        "x": a["x"].reshape(TILES, P, D).transpose(1, 0, 2).reshape(P, TILES * D),
        "ctxT": ctx.transpose(0, 2, 1),
        "ctxN": ctx[:, :full].reshape(BATCHES, FULL_KT, P, D).transpose(0, 2, 1, 3).reshape(BATCHES, P, full),
        "ctxTail": ctx[:, full:],
        "wq": a["L0_xattn_Wq"],
        "wk": a["L0_xattn_Wk"],
        "wvT": a["L0_xattn_Wv"].T,
        "wgT": a["L0_ffn_w_gate"].T,
        "w1T": np.concatenate([a["L0_ffn_w1_e"].reshape(-1, D).T, a["L0_ffn_w1_s"].T], axis=1),
        "w3T": np.concatenate([a["L0_ffn_w3_e"].reshape(-1, D).T, a["L0_ffn_w3_s"].T], axis=1),
        "w2T": np.concatenate([a["L0_ffn_w2_e"].transpose(0, 2, 1).reshape(-1, D), a["L0_ffn_w2_s"].T], axis=0)
                 .reshape(FT, P, D).transpose(1, 0, 2).reshape(P, FT * D),
        "g_xattn": a["g_xattn"].reshape(1, 1),
        "g_ffn": a["g_ffn"].reshape(1, 1),
    }
    arrays = {f"in_{k}": np.ascontiguousarray(v) for k, v in arrays.items()}
    nc = bacc.Bacc("TRN2", target_bir_lowering=False, num_devices=1)
    args = [nc.dram_tensor(k, v.shape, mybir.dt.from_np(v.dtype), kind="ExternalInput").ap()
            for k, v in arrays.items()]
    args.append(nc.dram_tensor("out_T", (D, TOKENS), F32, kind="ExternalOutput").ap())
    build(nc, *args)
    r = run_bass_kernel_spmd(nc, [arrays], core_ids=[0])
    return r.results[0]["out_T"].T.reshape(BATCHES, SEQ, D)
```

```python
from contextlib import ExitStack

import concourse.bass as bass
from concourse import mybir

P = 128
D = 128
BATCHES = 4
SEQ = 256
KEYS = 1601
EXPERTS = 16
GROUPS = 4
HIDDEN = 64
TOPK = 4
EPS = 1e-5

QT = SEQ // P
TILES = BATCHES * QT
TOKENS = BATCHES * SEQ
KT = -(-KEYS // P)
FULL_KT = KEYS // P
TAIL = KEYS - FULL_KT * P
KEYS_EVEN = KEYS + KEYS % 2
PAIRS = -(-KT // 2)
BANK = 512
BANKS = 4
SEG = KEYS // BANKS // 2 * 2
CHUNK_BANKS = ((0, 1), (2, 2), (3, 3))
CHUNKS = tuple((a * SEG, (z + 1) * SEG if z < BANKS - 1 else KEYS) for a, z in CHUNK_BANKS)
NCH = len(CHUNKS)
HALVES = 2
HTOK = TOKENS // HALVES
HTILES = TILES // HALVES
FT = EXPERTS * HIDDEN // P + 1
WCOLS = FT * P
STEPS = HALVES * FT
END_STEPS = 2
PIECES = 2
PT_RING = 3
Z_RING = 3
SPLIT_RING = 4
LAG = 3
TURN_Y3 = 4
LOGITS3 = TURN_Y3 + 1
WARM = (8, 2, 1)

ALU = mybir.AluOpType
ACT = mybir.ActivationFunctionType
AX = mybir.AxisListType
F32 = mybir.dt.float32
F32R = mybir.dt.float32r


def build(nc, x, ctxT, ctxN, ctxTail, wq, wk, wvT, wgT, w1T, w3T, w2T, g_xattn, g_ffn, outT):
    with ExitStack() as stack:
        def sb(name, shape, dt=F32):
            return stack.enter_context(nc.sbuf_tensor(name, shape, dt))

        def sem(name):
            return stack.enter_context(nc.semaphore(name))

        ident = sb("ident", [P, P])
        neghalf = sb("neghalf", [P, TILES])
        x_sb = sb("x_sb", [P, TILES, D])
        wq_sb = sb("wq_sb", [P, D])
        wk_sb = sb("wk_sb", [P, D])
        wv_sb = sb("wv_sb", [P, D])
        wqk = sb("wqk", [P, D])
        gates = sb("gates", [P, 2])
        tgates = sb("tgates", [P, 2])
        scrap = sb("scrap", [P, 1])
        stats = sb("stats", [P, TILES, 6])
        meanvar = sb("meanvar", [P, TILES, 2])
        vareps = sb("vareps", [P, TILES])
        rstd = sb("rstd", [P, TILES])
        xn = sb("xn", [P, TILES, D])
        xnT = sb("xnT", [P, TOKENS])
        q_hi = sb("q_hi", [P, TOKENS], F32R)
        q_lo = sb("q_lo", [P, TOKENS], F32R)
        cT = sb("cT", [P, 2, KEYS])
        cT_hi = sb("cT_hi", [P, 2, KEYS_EVEN], F32R)
        cT_lo = sb("cT_lo", [P, 2, KEYS_EVEN], F32R)
        cN = sb("cN", [P, BATCHES, KT * D])
        probs = sb("probs", [P, 2, QT, KEYS])
        pT = sb("pT", [P, PT_RING, BANK])
        chunk_max = sb("chunk_max", [P, TILES, NCH])
        neg_max = sb("neg_max", [P, TILES])
        chunk_sum = sb("chunk_sum", [P, TILES, NCH])
        row_sum = sb("row_sum", [P, TILES])
        inv_sum = sb("inv_sum", [P, TILES])
        attn_scale = sb("attn_scale", [P, TILES])
        oT = sb("oT", [P, SEQ])
        x1 = sb("x1", [P, TILES, D])
        stats2 = sb("stats2", [P, TILES, 6])
        meanvar2 = sb("meanvar2", [P, TILES, 2])
        vareps2 = sb("vareps2", [P, TILES])
        rstd2 = sb("rstd2", [P, TILES])
        y = sb("y", [P, QT, D])
        x1T = sb("x1T", [P, TOKENS])
        yT_hi = sb("yT_hi", [P, TOKENS], F32R)
        yT_lo = sb("yT_lo", [P, TOKENS], F32R)
        wg = sb("wg", [P, EXPERTS])
        wg_hi = sb("wg_hi", [P, EXPERTS], F32R)
        wg_lo = sb("wg_lo", [P, EXPERTS], F32R)
        w_raw = sb("w_raw", [P, 2, WCOLS])
        w_hi = sb("w_hi", [P, 3, WCOLS], F32R)
        w_lo = sb("w_lo", [P, 3, WCOLS], F32R)
        logit_sb = sb("logit_sb", [P, TILES, EXPERTS])
        expneg = sb("expneg", [P, HTILES, EXPERTS])
        comb = sb("comb", [P, HTILES, P])
        combT = sb("combT", [P, TOKENS], F32R)
        sel = sb("sel", [P, EXPERTS * HIDDEN], F32R)
        z_hi = sb("z_hi", [P, SPLIT_RING, BANK], F32R)
        z_lo = sb("z_lo", [P, SPLIT_RING, BANK], F32R)
        r_den = sb("r_den", [P, HTILES, EXPERTS])
        r_sig = sb("r_sig", [P, HTILES, EXPERTS])
        r_masked = sb("r_masked", [P, HTILES, EXPERTS + TOPK])
        r_pair = sb("r_pair", [P, HTILES * GROUPS, 6])
        r_group = sb("r_group", [P, HTILES, GROUPS])
        r_ahead = sb("r_ahead", [P, HTILES, GROUPS, 2, GROUPS])
        r_order = sb("r_order", [P, HTILES, GROUPS, 2, GROUPS])
        r_rank = sb("r_rank", [P, HTILES, GROUPS])
        r_top = sb("r_top", [P, HTILES, 8])
        r_rest = sb("r_rest", [P, HTILES, EXPERTS + TOPK])
        r_w = sb("r_w", [P, HTILES, EXPERTS])
        r_wsum = sb("r_wsum", [P, HTILES])
        r_winv = sb("r_winv", [P, HTILES])

        early = probs[:, 0, :, :].rearrange("p a b -> p (a b)")
        silu = [early[:, k * BANK:(k + 1) * BANK] for k in (0, 1)]
        gated = [early[:, k * BANK:(k + 1) * BANK] for k in (2, 3)]
        z = [early[:, k * BANK:(k + 1) * BANK] for k in (4, 5)] + [cT[:, 0, 0:BANK]]
        out_sb = xnT
        sel_raw = xn[:, :, :].rearrange("p a b -> p (a b)")

        ps_s = stack.enter_context(nc.psum_tensor("ps_s", [P, 4, BANK], F32))
        ps_x = stack.enter_context(nc.psum_tensor("ps_x", [P, 4, BANK], F32))
        ps_t = ps_x[:, 0:2, :]
        ps_o = ps_x[:, 2, :]
        ps_m = ps_x[:, 3, :]
        h1 = [ps_s[:, 0, :], ps_s[:, 1, :]]
        h3 = [ps_s[:, 2, :], ps_s[:, 3, :]]
        spread = [ps_t[:, 0, :], ps_t[:, 1, :]]
        acc = [ps_o, ps_m]

        l_wq, l_wv, l_wg, l_gate = (sem(n) for n in ("l_wq", "l_wv", "l_wg", "l_gate"))
        l_x = [sem(f"l_x{k}") for k in range(3)]
        l_cT_first = [sem(f"l_cT_first{k}") for k in range(NCH)]
        l_cT = [sem(f"l_cT{k}") for k in range(BATCHES)]
        l_cN = [sem(f"l_cN{k}") for k in range(BATCHES)]
        l_w = [sem(f"l_w{k}") for k in range(3)]
        s_fill = sem("s_fill")
        s_ident = sem("s_ident")
        s_tailz = sem("s_tailz")
        s_consts = sem("s_consts")
        s_sel = sem("s_sel")
        s_tg = sem("s_tg")
        s_wqk = sem("s_wqk")
        s_wqk_sb = sem("s_wqk_sb")
        s_var = sem("s_var")
        s_rstd = sem("s_rstd")
        s_xn = sem("s_xn")
        s_xT = sem("s_xT")
        s_xT_sb = sem("s_xT_sb")
        s_q = sem("s_q")
        s_qhi = sem("s_qhi")
        s_qlo = sem("s_qlo")
        s_cThi = sem("s_cThi")
        s_cTlo0 = sem("s_cTlo0")
        s_cTlo = sem("s_cTlo")
        s_score = sem("s_score")
        s_cmax = sem("s_cmax")
        s_max = sem("s_max")
        s_exp = sem("s_exp")
        s_turn = sem("s_turn")
        s_pT = {"act": sem("s_pT_act"), "dve": sem("s_pT_dve")}
        s_pv = sem("s_pv")
        s_oT = sem("s_oT")
        s_attn = sem("s_attn")
        s_scale = sem("s_scale")
        s_x1 = sem("s_x1")
        s_var2 = sem("s_var2")
        s_rstd2 = sem("s_rstd2")
        s_y = sem("s_y")
        s_yT = sem("s_yT")
        s_yTact = sem("s_yTact")
        s_yTlo = sem("s_yTlo")
        s_st = sem("s_st")
        s_whi = sem("s_whi")
        s_wlo = sem("s_wlo")
        s_wghi = sem("s_wghi")
        s_wglo = sem("s_wglo")
        s_logit = sem("s_logit")
        s_logit_sb = sem("s_logit_sb")
        s_expneg = sem("s_expneg")
        s_route = sem("s_route")
        s_comb = sem("s_comb")
        s_combT = sem("s_combT")
        s_combT_sb = sem("s_combT_sb")
        s_h1 = sem("s_h1")
        s_h3 = sem("s_h3")
        s_spread = sem("s_spread")
        s_silu = sem("s_silu")
        s_gated = sem("s_gated")
        s_z = sem("s_z")
        s_zhi = sem("s_zhi")
        s_zlo = sem("s_zlo")
        s_down = sem("s_down")
        s_out = sem("s_out")
        l_out = sem("l_out")

        group_tiles = (range(0, QT), range(QT, 2 * QT), range(2 * QT, TILES))
        NGROUP = len(group_tiles)
        turned_at = (ps_t[:, 0, :], ps_m, ps_m)
        query_at = (ps_t[:, 1, :], ps_m, ps_m)

        def group_cols(k):
            return slice(group_tiles[k][0] * P, (group_tiles[k][-1] + 1) * P)

        def scores_of(s):
            return ps_x if s == 1 else ps_s

        def chunk_scores(s, c):
            a, z = CHUNK_BANKS[c]
            return scores_of(s)[:, a:z + 1, 0:SEG if z < BANKS - 1 else KEYS - a * SEG]

        def chunk_of_bank(k):
            return [a <= k <= z for a, z in CHUNK_BANKS].index(True)

        def pairs_of(b, qt):
            first = PAIRS * (b - 1)
            if b == 0:
                return [], []
            if qt == 0:
                return [first], [first + 1, first + 2]
            return [first + 3], [first + 4, first + 5, first + 6]

        def pair_tiles(g):
            p = g % PAIRS
            return [t for t in (2 * p, 2 * p + 1) if t < KT]

        def mover(g):
            by_act = [k % PAIRS in (0, 1, 3, 4) for k in range(g + 1)]
            return ("act", sum(by_act)) if by_act[-1] else ("dve", g + 1 - sum(by_act))

        def pair_moved(eng, g):
            who, n = mover(g)
            eng.wait_ge(s_pT[who], n)

        def rows(t):
            return P if t < FULL_KT else TAIL

        def chunk_of(t):
            return chunk_of_bank(min((t * P + rows(t) - 1) // SEG, BANKS - 1))

        def is_shared(i):
            return i % FT == 0

        def w_tile(i):
            t = FT - 1 if is_shared(i) else i % FT - 1
            return slice(t * P, (t + 1) * P)

        def routed_steps(i):
            return i + 1 - (i // FT + 1)

        def pieces(i):
            w = HTOK if i < STEPS - 1 else HTOK // PIECES
            return [slice(a, a + w) for a in range(0, HTOK, w)]

        block = stack.enter_context(nc.Block())

        @block.sync
        def _(sp):
            def load_x(k):
                a, e = group_tiles[k][0], group_tiles[k][-1] + 1
                sp.dma_start(x_sb[:, a:e, :], x[:, a * D:e * D]).then_inc(l_x[k], 16)

            load_x(0)
            for c, (a, e) in enumerate(CHUNKS):
                sp.dma_start(cT[:, 0, a:e], ctxT[0][:, a:e]).then_inc(l_cT_first[c], 16)
                if c == 0:
                    load_x(1)
            sp.dma_start(cT[:, 1, :], ctxT[1]).then_inc(l_cT[1], 16)
            load_x(2)
            for b in range(BATCHES):
                if b >= 2:
                    sp.wait_ge(s_cThi, NCH * (b - 1))
                    if b == 2:
                        sp.wait_ge(s_cTlo0, NCH)
                    else:
                        sp.wait_ge(s_cTlo, NCH * (b - 2))
                    sp.dma_start(cT[:, b % 2, :], ctxT[b]).then_inc(l_cT[b], 16)
                sp.dma_start(cN[:, b, 0:FULL_KT * D], ctxN[b]).then_inc(l_cN[b], 16)
                sp.dma_start(cN[0:TAIL, b, FULL_KT * D:KT * D], ctxTail[b]).then_inc(l_cN[b], 16)
                if b == 0:
                    sp.dma_start(gates[:, 0:1], g_xattn.broadcast_to([P, 1])).then_inc(l_gate, 16)
                    sp.dma_start(gates[:, 1:2], g_ffn.broadcast_to([P, 1])).then_inc(l_gate, 16)
                if b == 1:
                    sp.dma_start(wv_sb[:, :], wvT).then_inc(l_wv, 16)
                    sp.dma_start(wg[:, :], wgT).then_inc(l_wg, 16)
                    for k, w in enumerate((w1T, w3T)):
                        sp.dma_start(w_raw[:, k, :], w).then_inc(l_w[k], 16)
            sp.wait_ge(s_wlo, 1)
            sp.dma_start(w_raw[:, 0, :], w2T).then_inc(l_w[2], 16)
            for n in range(PIECES * HALVES):
                sp.wait_ge(s_out, n + 1)
                w = HTOK // PIECES
                sp.dma_start(outT[:, n * w:(n + 1) * w], out_sb[:, n * w:(n + 1) * w]).then_inc(l_out, 16)
            sp.wait_ge(l_out, 16 * PIECES * HALVES)

        @block.gpsimd
        def _(pool):
            nc.gpsimd.memset(ident[:, :], 1.0).then_inc(s_fill, 1)
            nc.gpsimd.memset(neghalf[:, :], -0.5).then_inc(s_fill, 1)
            pool.wait_ge(s_fill, 2)
            nc.gpsimd.affine_select(out=ident[:, :], in_=ident[:, :], compare_op=ALU.is_equal, fill=0.0,
                                    base=0, pattern=[[-1, P]], channel_multiplier=1).then_inc(s_ident, 1)

            def rsqrt(var, out, tiles, ready, n, done):
                pool.wait_ge(ready, n)
                a, b = tiles[0], tiles[-1] + 1
                nc.gpsimd.tensor_tensor(out[:, a:b], var[:, a:b], neghalf[:, a:b], ALU.pow).then_inc(done, 1)

            rsqrt(vareps, rstd, group_tiles[0], s_var, 1, s_rstd)
            rsqrt(vareps, rstd, group_tiles[1], s_var, 2, s_rstd)

            def cT_low(b, c):
                a, e = CHUNKS[c]
                pool.wait_ge(s_cThi, NCH * b + c + 1)
                if b >= 2:
                    pool.wait_ge(s_score, NCH * QT * (b - 1))
                nc.gpsimd.tensor_tensor(cT_lo[:, b % 2, a:e], cT[:, b % 2, a:e],
                                        cT_hi[:, b % 2, a:e].bitcast(F32), ALU.subtract).then_inc(s_cTlo, 1)

            def w_low(k):
                pool.wait_ge(s_whi, k + 1)
                nc.gpsimd.tensor_tensor(w_lo[:, k, :], w_raw[:, k % 2, :], w_hi[:, k, :].bitcast(F32),
                                        ALU.subtract).then_inc(s_wlo, 1)

            def batch_rsqrt2(j):
                rsqrt(vareps2, rstd2, range(QT * j, QT * j + QT), s_var2, j + 1, s_rstd2)

            for c in range(NCH):
                cT_low(1, c)
            rsqrt(vareps, rstd, group_tiles[2], s_var, 3, s_rstd)
            for c in range(NCH):
                cT_low(2, c)
            sel3 = sel_raw.rearrange("p (e f) -> p e f", f=HIDDEN)
            pool.wait_ge(s_xT, NGROUP)
            nc.gpsimd.memset(sel_raw, 0.0).then_inc(s_fill, 1)
            pool.wait_ge(s_fill, 3)
            nc.gpsimd.affine_select(out=sel3, in_=sel3, compare_op=ALU.not_equal, fill=1.0, base=0,
                                    pattern=[[-1, EXPERTS], [0, HIDDEN]], channel_multiplier=1).then_inc(s_fill, 1)
            pool.wait_ge(s_fill, 4)
            nc.gpsimd.affine_select(out=sel3, in_=sel3, compare_op=ALU.not_equal, fill=1.0, base=-EXPERTS,
                                    pattern=[[-1, EXPERTS], [0, HIDDEN]], channel_multiplier=1).then_inc(s_fill, 1)
            w_low(0)
            cT_low(3, 0)
            batch_rsqrt2(0)
            for c in range(1, NCH):
                cT_low(3, c)
            w_low(1)
            batch_rsqrt2(1)
            w_low(2)
            batch_rsqrt2(2)
            for i in range(STEPS - END_STEPS):
                pool.wait_ge(s_zhi, i + 1)
                k = i % SPLIT_RING
                if i >= SPLIT_RING:
                    pool.wait_ge(s_down, i - SPLIT_RING + 1)
                nc.gpsimd.tensor_tensor(z_lo[:, k, :], z[i % Z_RING], z_hi[:, k, :].bitcast(F32),
                                        ALU.subtract).then_inc(s_zlo, 1)
                if i == 0:
                    batch_rsqrt2(3)

        @block.scalar
        def _(act):
            act.dma_start(wq_sb[:, :], wq).then_inc(l_wq, 16)
            act.dma_start(wk_sb[:, :], wk).then_inc(l_wq, 16)

            def cT_high(b, c):
                a, e = CHUNKS[c]
                act.wait_ge(l_cT_first[c] if b == 0 else l_cT[b], 16)
                if b >= 2:
                    act.wait_ge(s_score, NCH * QT * (b - 1))
                nc.scalar.copy(cT_hi[:, b % 2, a:e], cT[:, b % 2, a:e]).then_inc(s_cThi, 1)

            def move_x(k):
                act.wait_ge(s_xT, k + 1)
                cols = group_cols(k)
                nc.scalar.copy(xnT[:, cols], turned_at[k][:, 0:cols.stop - cols.start]).then_inc(s_xT_sb, 1)

            def q_high(k):
                act.wait_ge(s_q, k + 1)
                cols = group_cols(k)
                nc.scalar.copy(q_hi[:, cols], query_at[k][:, 0:cols.stop - cols.start]).then_inc(s_qhi, 1)

            def exponential(b, qt, c):
                s = QT * b + qt
                a, e = CHUNKS[c]
                act.wait_ge(s_max, s + 1)
                if b >= 2:
                    act.wait_ge(s_turn, PAIRS * (b - 1))
                banks = CHUNK_BANKS[c][1] - CHUNK_BANKS[c][0] + 1
                nc.scalar.activation(probs[:, b % 2, qt, a:e].rearrange("p (k w) -> p k w", k=banks),
                                     chunk_scores(s, c), ACT.Exp, bias=neg_max[:, s:s + 1],
                                     accum_out=chunk_sum[:, s, c:c + 1]).then_inc(s_exp, 1)

            def move_pair(g):
                if mover(g)[0] != "act":
                    return
                w = len(pair_tiles(g)) * SEQ
                r = rows(pair_tiles(g)[-1])
                act.wait_ge(s_turn, g + 1)
                if g >= PT_RING:
                    act.wait_ge(s_pv, g - PT_RING + 1)
                nc.scalar.copy(pT[0:r, g % PT_RING, 0:w], ps_t[0:r, g % 2, 0:w]).then_inc(s_pT["act"], 1)

            def move_o(j):
                act.wait_ge(s_pv, PAIRS * (j + 1))
                if j >= 1:
                    act.wait_ge(s_attn, j)
                nc.scalar.copy(oT[:, :], ps_o[:, 0:SEQ]).then_inc(s_oT, 1)

            def move_y(j):
                a = SEQ * j
                act.wait_ge(s_yT, j + 1)
                nc.scalar.copy(yT_hi[:, a:a + SEQ], ps_m[:, 0:SEQ]).then_inc(s_yTact, 1)
                nc.scalar.copy(x1T[:, a:a + SEQ], ps_m[:, SEQ:2 * SEQ]).then_inc(s_yTact, 1)

            def move_logits(j):
                act.wait_ge(s_logit, j + 1)
                nc.scalar.copy(logit_sb[:, QT * j:QT * j + QT, :].rearrange("p a b -> p (a b)"),
                               ps_m[:, 0:QT * EXPERTS]).then_inc(s_logit_sb, 1)

            def exp_logits(h):
                act.wait_ge(s_logit_sb, QT * (h + 1))
                if h >= 1:
                    act.wait_ge(s_comb, h)
                nc.scalar.activation(expneg[:], logit_sb[:, HTILES * h:HTILES * (h + 1), :], ACT.Exp,
                                     scale=-1.0).then_inc(s_expneg, 1)

            cT_high(0, 0)
            act.wait_ge(s_wqk, 1)
            nc.scalar.copy(wqk[:, :], ps_m[:, 0:D]).then_inc(s_wqk_sb, 1)
            move_x(0)
            q_high(0)
            cT_high(0, 1)
            cT_high(0, 2)
            move_x(1)
            q_high(1)
            for c in range(NCH):
                cT_high(1, c)

            def silu_of(i):
                act.wait_ge(s_h1, i + 1)
                if i == 0:
                    act.wait_ge(s_turn, PAIRS * (BATCHES - 1))
                if i >= 2:
                    act.wait_ge(s_z, i - 1)
                for m in pieces(i):
                    nc.scalar.activation(silu[i % 2][:, m], h1[i % 2][:, m], ACT.Silu).then_inc(s_silu, 1)

            def z_high(i):
                act.wait_ge(s_z, i + 1)
                if i >= SPLIT_RING:
                    act.wait_ge(s_down, i - SPLIT_RING + 1)
                nc.scalar.copy(z_hi[:, i % SPLIT_RING, :], z[i % Z_RING]).then_inc(s_zhi, 1)

            def move_comb(h):
                act.wait_ge(s_combT, h + 1)
                nc.scalar.copy(combT[:, h * HTOK:(h + 1) * HTOK], ps_t[:, 0, :]).then_inc(s_combT_sb, 1)

            for b in range(BATCHES):
                for qt in range(QT):
                    before, after = pairs_of(b, qt)
                    if b == 1 and qt == 0:
                        act.wait_ge(l_gate, 32)
                        nc.scalar.activation(tgates[:, :], gates[:, :], ACT.Tanh).then_inc(s_tg, 1)
                    for g in before:
                        move_pair(g)
                    if b == 1 and qt == 1:
                        move_x(2)
                    if b == 3 and qt == 0:
                        move_logits(0)
                    for g in after[:1]:
                        move_pair(g)
                    if b == 1 and qt == 1:
                        q_high(2)
                    if b >= 2 and qt == 0:
                        move_o(b - 2)
                    for c in range(NCH):
                        exponential(b, qt, c)
                        if 1 + c < len(after):
                            move_pair(after[1 + c])
                    if qt == 0 and 1 <= b < BATCHES - 1:
                        for c in range(NCH):
                            cT_high(b + 1, c)
                    if b >= 2 and qt == 1:
                        move_y(b - 2)
            first = PAIRS * (BATCHES - 1)
            move_pair(first)
            move_logits(1)
            move_pair(first + 1)
            exp_logits(0)
            move_o(2)
            silu_of(0)
            move_pair(first + 3)
            silu_of(1)
            move_pair(first + 4)
            move_y(2)
            z_high(0)
            move_logits(2)
            move_o(3)
            move_comb(0)
            for i in range(2, STEPS):
                if i == TURN_Y3:
                    move_y(3)
                silu_of(i)
                if i == LOGITS3:
                    nc.scalar.activation(scrap[:, :], tgates[:, 0:1], ACT.Exp)
                    move_logits(3)
                    exp_logits(1)
                if i - 1 < STEPS - END_STEPS:
                    z_high(i - 1)
                if i == FT:
                    move_comb(1)

        @block.vector
        def _(dve):
            steps = [0]

            def link(ins):
                steps[0] += 1
                ins.then_inc(s_st, 1)
                dve.wait_ge(s_st, steps[0])

            routed = [0]

            def route(ins):
                routed[0] += 1
                ins.then_inc(s_route, 1)
                dve.wait_ge(s_route, routed[0])

            def norm_stats(src, st, mv, var, tiles, done):
                for t in tiles:
                    ins = nc.vector.bn_stats(st[:, t, :], src[:, t, :])
                link(ins)
                for t in tiles:
                    ins = nc.vector.bn_aggr(mv[:, t, :], st[:, t, :])
                link(ins)
                a, b = tiles[0], tiles[-1] + 1
                nc.vector.tensor_scalar(var[:, a:b], mv[:, a:b, 1], EPS, None, ALU.add).then_inc(done, 1)

            def x_stats(k):
                dve.wait_ge(l_x[k], 16)
                norm_stats(x_sb, stats, meanvar, vareps, group_tiles[k], s_var)

            def norm_x(k):
                dve.wait_ge(s_rstd, k + 1)
                for t in group_tiles[k]:
                    ins = nc.vector.tensor_scalar(xn[:, t, :], x_sb[:, t, :], meanvar[:, t, 0:1], rstd[:, t:t + 1],
                                                  ALU.subtract, ALU.mult)
                    ins.then_inc(s_xn, 1)

            def q_low(k):
                dve.wait_ge(s_qhi, k + 1)
                cols = group_cols(k)
                nc.vector.tensor_tensor(q_lo[:, cols], query_at[k][:, 0:cols.stop - cols.start],
                                        q_hi[:, cols].bitcast(F32), ALU.subtract).then_inc(s_qlo, 1)

            def cT_low0(c):
                a, e = CHUNKS[c]
                dve.wait_ge(s_cThi, c + 1)
                nc.vector.tensor_tensor(cT_lo[:, 0, a:e], cT[:, 0, a:e], cT_hi[:, 0, a:e].bitcast(F32),
                                        ALU.subtract).then_inc(s_cTlo0, 1)

            def w_high(k):
                dve.wait_ge(l_w[k], 16)
                nc.vector.tensor_copy(w_hi[:, k, :], w_raw[:, k % 2, :]).then_inc(s_whi, 1)

            def chunk_maximum(b, qt, c):
                s = QT * b + qt
                dve.wait_ge(s_score, NCH * s + c + 1)
                nc.vector.tensor_reduce(chunk_max[:, s, c:c + 1], chunk_scores(s, c), AX.XY,
                                        ALU.max).then_inc(s_cmax, 1)

            def maximum(b, qt):
                s = QT * b + qt
                dve.wait_ge(s_cmax, NCH * (s + 1))
                nc.vector.tensor_reduce(neg_max[:, s:s + 1], chunk_max[:, s, :], AX.X, ALU.max,
                                        negate=True).then_inc(s_max, 1)

            def move_pair(g):
                if mover(g)[0] != "dve":
                    return
                w = len(pair_tiles(g)) * SEQ
                r = rows(pair_tiles(g)[-1])
                dve.wait_ge(s_turn, g + 1)
                if g >= PT_RING:
                    dve.wait_ge(s_pv, g - PT_RING + 1)
                nc.vector.tensor_copy(pT[0:r, g % PT_RING, 0:w], ps_t[0:r, g % 2, 0:w]).then_inc(s_pT["dve"], 1)

            def attention_scale(j):
                a, e = QT * j, QT * j + QT
                dve.wait_ge(s_exp, NCH * e)
                link(nc.vector.tensor_reduce(row_sum[:, a:e], chunk_sum[:, a:e, :], AX.X, ALU.add))
                link(nc.vector.reciprocal(inv_sum[:, a:e], row_sum[:, a:e]))
                dve.wait_ge(s_tg, 1)
                link(nc.vector.tensor_scalar(attn_scale[:, a:e], inv_sum[:, a:e], tgates[:, 0:1], None, ALU.mult))

            def residual(j):
                a, e = QT * j, QT * j + QT
                dve.wait_ge(s_attn, j + 1)
                for t in range(a, e):
                    ins = nc.vector.scalar_tensor_tensor(out=x1[:, t, :], in0=ps_m[:, (t - a) * D:(t - a + 1) * D],
                                                         scalar=attn_scale[:, t:t + 1], in1=x_sb[:, t, :],
                                                         op0=ALU.mult, op1=ALU.add)
                    ins.then_inc(s_x1, 1)
                dve.wait_ge(s_x1, e)
                norm_stats(x1, stats2, meanvar2, vareps2, range(a, e), s_var2)

            def norm_y(j):
                a = QT * j
                dve.wait_ge(s_rstd2, j + 1)
                if j >= 1:
                    dve.wait_ge(s_yT, j)
                for t in range(a, a + QT):
                    nc.vector.tensor_scalar(y[:, t - a, :], x1[:, t, :], meanvar2[:, t, 0:1], rstd2[:, t:t + 1],
                                            ALU.subtract, ALU.mult).then_inc(s_y, 1)

            def yT_low(j):
                a = SEQ * j
                dve.wait_ge(s_yTact, 2 * (j + 1))
                nc.vector.tensor_tensor(yT_lo[:, a:a + SEQ], ps_m[:, 0:SEQ], yT_hi[:, a:a + SEQ].bitcast(F32),
                                        ALU.subtract).then_inc(s_yTlo, 1)

            def bc(v, n):
                return v.unsqueeze(len(v.shape)).broadcast_to(list(v.shape) + [n])

            def router_constants():
                nc.vector.memset(comb[:], 0.0)
                link(nc.vector.memset(r_order[:], 0.0))
                for g in range(1, GROUPS):
                    nc.vector.memset(r_order[:, :, g - 1, 0, g:GROUPS], 1.0)
                    nc.vector.memset(r_order[:, :, g, 1, 0:g], 1.0)
                for k in range(TOPK):
                    ins = nc.vector.memset(r_masked[:, :, EXPERTS + k:EXPERTS + k + 1], -1.0 - k)
                ins.then_inc(s_consts, 1)

            def router(h, part):
                if part == 0:
                    dve.wait_ge(s_expneg, h + 1)
                    route(nc.vector.tensor_scalar(r_den[:], expneg[:], 1.0, None, ALU.add))
                    route(nc.vector.reciprocal(r_sig[:], r_den[:]))
                    sg = r_sig[:].rearrange("p t (g m) -> p (t g) m", g=GROUPS)
                    nc.vector.tensor_tensor(r_pair[:, :, 0:2], sg[:, :, 0:2], sg[:, :, 2:4], ALU.add)
                    nc.vector.tensor_tensor(r_pair[:, :, 2:4], sg[:, :, 0:4:2], sg[:, :, 1:4:2], ALU.add)
                    nc.vector.tensor_tensor(r_pair[:, :, 4:5], sg[:, :, 0:1], sg[:, :, 3:4], ALU.add)
                    route(nc.vector.tensor_tensor(r_pair[:, :, 5:6], sg[:, :, 1:2], sg[:, :, 2:3], ALU.add))
                    route(nc.vector.tensor_reduce(r_group[:].rearrange("p t g -> p (t g)"), r_pair[:], AX.X, ALU.max))
                if part == 1:
                    dve.wait_ge(s_consts, 1)
                    mine = r_group[:].unsqueeze(3).broadcast_to([P, HTILES, GROUPS, GROUPS])
                    other = r_group[:].unsqueeze(2).broadcast_to([P, HTILES, GROUPS, GROUPS])
                    nc.vector.tensor_tensor(r_ahead[:, :, :, 0, :], other, mine, ALU.is_gt)
                    route(nc.vector.tensor_tensor(r_ahead[:, :, :, 1, :], other, mine, ALU.is_ge))
                    flat = "p t g a b -> p (t g a b)"
                    route(nc.vector.tensor_tensor(r_ahead[:].rearrange(flat), r_ahead[:].rearrange(flat),
                                                  r_order[:].rearrange(flat), ALU.mult))
                    route(nc.vector.tensor_reduce(r_rank[:].rearrange("p t g -> p (t g)"),
                                                  r_ahead[:].rearrange("p t g a b -> p (t g) (a b)"), AX.X, ALU.add))
                    n = EXPERTS // GROUPS
                    for t in range(HTILES):
                        ins = nc.vector.scalar_tensor_tensor(
                            out=r_masked[:, t, 0:EXPERTS].rearrange("p (g m) -> p g m", m=n),
                            in0=bc(r_rank[:, t, :], n), scalar=1.5,
                            in1=r_sig[:, t, :].rearrange("p (g m) -> p g m", m=n), op0=ALU.is_lt, op1=ALU.mult)
                    route(ins)
                if part == 2:
                    for t in range(HTILES):
                        ins = nc.vector.max(r_top[:, t, :], r_masked[:, t, 0:EXPERTS])
                    route(ins)
                    nc.vector.tensor_reduce(r_wsum[:], r_top[:, :, 0:TOPK], AX.X, ALU.add)
                    route(nc.vector.tensor_copy(r_top[:, :, TOPK:2 * TOPK], r_masked[:, :, EXPERTS:EXPERTS + TOPK]))
                    nc.vector.tensor_scalar(r_wsum[:], r_wsum[:], 1e-6, None, ALU.add)
                    for t in range(HTILES):
                        ins = nc.vector.match_replace(r_rest[:, t, :], r_top[:, t, :], r_masked[:, t, :], 0.0)
                    route(ins)
                if part == 3:
                    nc.vector.reciprocal(r_winv[:], r_wsum[:])
                    route(nc.vector.tensor_tensor(r_w[:], r_masked[:, :, 0:EXPERTS], r_rest[:, :, 0:EXPERTS],
                                                  ALU.subtract))
                    if h >= 1:
                        dve.wait_ge(s_combT, h)
                    nc.vector.tensor_tensor(comb[:, :, 0:EXPERTS].bitcast(F32R), r_w[:], bc(r_winv[:], EXPERTS),
                                            ALU.mult)
                    route(nc.vector.tensor_tensor(r_w[:], r_w[:], bc(r_winv[:], EXPERTS), ALU.mult))
                    nc.vector.tensor_tensor(comb[:, :, EXPERTS:2 * EXPERTS], r_w[:], comb[:, :, 0:EXPERTS],
                                            ALU.subtract).then_inc(s_comb, 1)

            nc.vector.memset(cT_hi[:, :, KEYS:KEYS_EVEN].bitcast(F32), 0.0).then_inc(s_tailz, 1)
            nc.vector.memset(cT_lo[:, :, KEYS:KEYS_EVEN].bitcast(F32), 0.0).then_inc(s_tailz, 1)
            router_constants()
            x_stats(0)
            norm_x(0)
            x_stats(1)
            cT_low0(0)
            norm_x(1)
            q_low(0)
            cT_low0(1)
            cT_low0(2)

            def gate(i):
                if i >= Z_RING:
                    done = min(i - Z_RING + 1, STEPS - END_STEPS)
                    dve.wait_ge(s_zhi, done)
                    dve.wait_ge(s_zlo, done)
                dve.wait_ge(s_h3, i + 1)
                for n, m in enumerate(pieces(i)):
                    dve.wait_ge(s_silu, i + n + 1)
                    if is_shared(i):
                        nc.vector.tensor_tensor(z[i % Z_RING][:, m], silu[i % 2][:, m], h3[i % 2][:, m],
                                                ALU.mult).then_inc(s_z, 1)
                    else:
                        nc.vector.tensor_tensor(gated[i % 2][:, m], silu[i % 2][:, m], h3[i % 2][:, m],
                                                ALU.mult).then_inc(s_gated, 1)

            def combine(i):
                if is_shared(i):
                    return
                for n, m in enumerate(pieces(i)):
                    dve.wait_ge(s_gated, routed_steps(i) + n)
                    dve.wait_ge(s_spread, routed_steps(i))
                    nc.vector.tensor_tensor(z[i % Z_RING][:, m], gated[i % 2][:, m], spread[i % 2][:, m],
                                            ALU.mult).then_inc(s_z, 1)

            def finish(h):
                w = HTOK // PIECES
                dve.wait_ge(s_down, STEPS - 1 + PIECES if h == HALVES - 1 else FT * (h + 1))
                for n in range(PIECES):
                    a = h * HTOK + n * w
                    nc.vector.scalar_tensor_tensor(out=out_sb[:, a:a + w], in0=acc[h][:, n * w:(n + 1) * w],
                                                   scalar=tgates[:, 1:2], in1=x1T[:, a:a + w],
                                                   op0=ALU.mult, op1=ALU.add).then_inc(s_out, 1)

            for b in range(BATCHES):
                for qt in range(QT):
                    before, after = pairs_of(b, qt)
                    chunk_maximum(b, qt, 0)
                    if b == 0 and qt == 0:
                        q_low(1)
                    chunk_maximum(b, qt, 1)
                    for g in before:
                        move_pair(g)
                    if b >= 2 and qt == 0:
                        attention_scale(b - 2)
                    if b >= 2 and qt == 1:
                        norm_y(b - 2)
                    chunk_maximum(b, qt, 2)
                    maximum(b, qt)
                    if b == 1 and qt == 0:
                        x_stats(2)
                    if b == 1 and qt == 1:
                        q_low(2)
                    for n, g in enumerate(after):
                        move_pair(g)
                        if n == 1 and b >= 2 and qt == 0:
                            residual(b - 2)
                    if b >= 2 and qt == 1:
                        yT_low(b - 2)
                    if b == 1 and qt == 0:
                        norm_x(2)
                    if qt == 1 and b >= 1:
                        w_high(b - 1)
                    if b == 2 and qt == 0:
                        dve.wait_ge(l_wg, 16)
                        nc.vector.tensor_copy(wg_hi[:, :], wg[:, :]).then_inc(s_wghi, 1)
                        dve.wait_ge(s_wghi, 1)
                        nc.vector.tensor_tensor(wg_lo[:, :], wg[:, :], wg_hi[:, :].bitcast(F32),
                                                ALU.subtract).then_inc(s_wglo, 1)
                    if b == 3 and qt == 0:
                        dve.wait_ge(s_fill, 5)
                        nc.vector.tensor_copy(sel[:, :], sel_raw).then_inc(s_sel, 1)
            first = PAIRS * (BATCHES - 1)
            attention_scale(2)
            attention_scale(3)
            router(0, 0)
            move_pair(first + 2)
            gate(0)
            residual(2)
            router(0, 1)
            norm_y(2)
            move_pair(first + 5)
            router(0, 2)
            move_pair(first + 6)
            yT_low(2)
            router(0, 3)
            for i in range(1, STEPS):
                if i != FT - 1:
                    gate(i)
                combine(i)
                if i == TURN_Y3 - 3:
                    residual(3)
                if i == TURN_Y3 - 2:
                    norm_y(3)
                if i == TURN_Y3 - 1:
                    yT_low(3)
                if i == LOGITS3:
                    router(1, 0)
                    router(1, 1)
                if i == LOGITS3 + 2:
                    gate(FT - 1)
                    router(1, 2)
                    router(1, 3)
                if i == FT + LAG:
                    finish(0)
            finish(1)

        @block.tensor
        def _(pe):
            def product(out, parts):
                lh, ll, rh, rl = parts
                nc.tensor.matmul(out, lh, rh, start=True, stop=False)
                nc.tensor.matmul(out, lh, rl, start=False, stop=False)
                return nc.tensor.matmul(out, ll, rh, start=False, stop=True)

            def turn_x(k):
                if k == 1:
                    pe.wait_ge(s_wqk_sb, 1)
                if k == 2:
                    pe.wait_ge(s_exp, NCH * QT)
                for n, t in enumerate(group_tiles[k]):
                    pe.wait_ge(s_xn, t + 1)
                    ins = nc.tensor.transpose(turned_at[k][:, n * P:(n + 1) * P], xn[:, t, :], ident[:, :])
                ins.then_inc(s_xT, 1)

            def query(k):
                pe.wait_ge(s_xT_sb, k + 1)
                cols = group_cols(k)
                nc.tensor.matmul(query_at[k][:, 0:cols.stop - cols.start], wqk[:, :], xnT[:, cols],
                                 start=True, stop=True).then_inc(s_q, 1)

            def score(b, qt, c):
                s = QT * b + qt
                if s == 1 and c == NCH - 1:
                    pe.wait_ge(s_qlo, 2)
                if s >= 2:
                    last = 0 if s == 2 else s - 1
                    pe.wait_ge(s_exp, NCH * last + c + 1)
                if c == 0 and qt == 0 and b < NGROUP:
                    pe.wait_ge(s_qhi, b + 1)
                    pe.wait_ge(s_qlo, b + 1)
                pe.wait_ge(s_cThi, NCH * b + c + 1)
                if b == 0:
                    pe.wait_ge(s_cTlo0, c + 1)
                else:
                    pe.wait_ge(s_cTlo, NCH * (b - 1) + c + 1)
                q = slice(s * P, (s + 1) * P)
                if s == 0 and c == 0:
                    pe.wait_ge(s_tailz, 2)
                for k in range(CHUNK_BANKS[c][0], CHUNK_BANKS[c][1] + 1):
                    m = slice(k * SEG, (k + 1) * SEG if k < BANKS - 1 else KEYS_EVEN)
                    ins = product(scores_of(s)[:, k, 0:m.stop - m.start],
                                  (q_hi[:, q], q_lo[:, q], cT_hi[:, b % 2, m], cT_lo[:, b % 2, m]))
                ins.then_inc(s_score, 1)

            def turn(g):
                b = g // PAIRS
                if g < 2:
                    pe.wait_ge(s_exp, NCH + chunk_of_bank(g) + 1)
                else:
                    pair_moved(pe, g - 2)
                for n, t in enumerate(pair_tiles(g)):
                    pe.wait_ge(s_exp, NCH * (QT * b + 1) + chunk_of(t) + 1)
                    for qt in range(QT):
                        o = (n * QT + qt) * P
                        ins = nc.tensor.transpose(ps_t[0:rows(t), g % 2, o:o + P],
                                                  probs[:, b % 2, qt, t * P:t * P + rows(t)], ident[:, :])
                ins.then_inc(s_turn, 1)

            def weigh(g):
                b = g // PAIRS
                if g % PAIRS == 0:
                    pe.wait_ge(l_cN[b], 32)
                    if b == 0:
                        pe.wait_ge(s_exp, NCH * QT)
                    else:
                        pe.wait_ge(s_oT, b)
                pair_moved(pe, g)
                for n, t in enumerate(pair_tiles(g)):
                    r = rows(t)
                    ins = nc.tensor.matmul(ps_o[:, 0:SEQ], cN[0:r, b, t * D:(t + 1) * D],
                                           pT[0:r, g % PT_RING, n * SEQ:(n + 1) * SEQ],
                                           start=(t == 0), stop=(t == KT - 1))
                ins.then_inc(s_pv, 1)

            def attend(j):
                pe.wait_ge(s_oT, j + 1)
                if j == 0:
                    pe.wait_ge(l_wv, 16)
                    pe.wait_ge(s_qlo, NGROUP)
                else:
                    pe.wait_ge(s_logit_sb, j)
                for qt in range(QT):
                    ins = nc.tensor.matmul(ps_m[:, qt * D:(qt + 1) * D], oT[:, qt * P:(qt + 1) * P], wv_sb[:, :],
                                           start=True, stop=True)
                ins.then_inc(s_attn, 1)

            def turn_y(j):
                pe.wait_ge(s_y, QT * (j + 1))
                for n in range(2 * QT):
                    src = y[:, n, :] if n < QT else x1[:, QT * j + n - QT, :]
                    ins = nc.tensor.transpose(ps_m[:, n * P:(n + 1) * P], src, ident[:, :])
                ins.then_inc(s_yT, 1)

            def logits(j):
                pe.wait_ge(s_yTact, 2 * (j + 1))
                pe.wait_ge(s_yTlo, j + 1)
                if j == 0:
                    pe.wait_ge(s_wghi, 1)
                    pe.wait_ge(s_wglo, 1)
                for qt in range(QT):
                    t = slice((QT * j + qt) * P, (QT * j + qt + 1) * P)
                    ins = product(ps_m[:, qt * EXPERTS:(qt + 1) * EXPERTS],
                                  (yT_hi[:, t], yT_lo[:, t], wg_hi[:, :], wg_lo[:, :]))
                ins.then_inc(s_logit, 1)

            def turn_comb(h):
                pe.wait_ge(s_comb, h + 1)
                if h == 0:
                    pair_moved(pe, PAIRS * BATCHES - 2)
                else:
                    pe.wait_ge(s_z, FT)
                for t in range(HTILES):
                    ins = nc.tensor.transpose(ps_t[:, 0, t * P:(t + 1) * P], comb[:, t, :], ident[:, :])
                ins.then_inc(s_combT, 1)

            def up(i):
                h = i // FT
                tok = slice(h * HTOK, (h + 1) * HTOK)
                if i == 0:
                    pe.wait_ge(s_exp, NCH * TILES)
                    pe.wait_ge(s_whi, 2)
                    pe.wait_ge(s_wlo, 2)
                    pe.wait_ge(s_yTlo, QT)
                if i >= 2:
                    pe.wait_ge(s_silu, i - 1)
                product(h1[i % 2], (w_hi[:, 0, w_tile(i)], w_lo[:, 0, w_tile(i)],
                                    yT_hi[:, tok], yT_lo[:, tok])).then_inc(s_h1, 1)
                if i >= 2 and is_shared(i - 2):
                    pe.wait_ge(s_z, i - 1)
                elif i >= 2:
                    pe.wait_ge(s_gated, routed_steps(i - 2))
                if i == STEPS - 1:
                    spread_weights(i)
                product(h3[i % 2], (w_hi[:, 1, w_tile(i)], w_lo[:, 1, w_tile(i)],
                                    yT_hi[:, tok], yT_lo[:, tok])).then_inc(s_h3, 1)

            def spread_weights(i):
                if is_shared(i):
                    return
                h = i // FT
                pe.wait_ge(s_combT_sb, h + 1)
                if i == 1:
                    pe.wait_ge(s_sel, 1)
                if i == 1:
                    pair_moved(pe, PAIRS * BATCHES - i)
                elif i > 2:
                    pe.wait_ge(s_z, i - 1)
                nc.tensor.matmul(spread[i % 2], sel[:, w_tile(i)], combT[:, h * HTOK:(h + 1) * HTOK],
                                 start=True, stop=True).then_inc(s_spread, 1)

            def down(i):
                h = i // FT
                if i == 0:
                    pe.wait_ge(s_whi, 3)
                    pe.wait_ge(s_wlo, 3)
                    pe.wait_ge(s_oT, BATCHES)
                if i == FT:
                    pe.wait_ge(s_logit_sb, BATCHES)
                first, last = i % FT == 0, i % FT == FT - 1
                if i >= STEPS - END_STEPS:
                    for n, m in enumerate(pieces(i)):
                        pe.wait_ge(s_z, i + n + 1)
                        nc.tensor.matmul(acc[h][:, m], w_raw[:, 0, w_tile(i)], z[i % Z_RING][:, m],
                                         start=False, stop=last and m.stop == HTOK).then_inc(s_down, 1)
                    return
                k = i % SPLIT_RING
                pe.wait_ge(s_zhi, i + 1)
                nc.tensor.matmul(acc[h][:, :], w_hi[:, 2, w_tile(i)], z_hi[:, k, :], start=first, stop=False)
                nc.tensor.matmul(acc[h][:, :], w_lo[:, 2, w_tile(i)], z_hi[:, k, :], start=False, stop=False)
                pe.wait_ge(s_zlo, i + 1)
                nc.tensor.matmul(acc[h][:, :], w_hi[:, 2, w_tile(i)], z_lo[:, k, :], start=False,
                                 stop=last).then_inc(s_down, 1)

            def unit(g):
                turn(g)
                if g >= 2:
                    weigh(g - 2)

            def warm(n):
                for _ in range(n):
                    nc.tensor.matmul(ps_s[:, 0, 0:P], ident[:, :], ident[:, :], start=True, stop=True)

            pe.wait_ge(s_ident, 1)
            warm(WARM[0])
            pe.wait_ge(l_wq, 32)
            nc.tensor.matmul(ps_m[:, 0:D], wq_sb[:, :], wk_sb[:, :], start=True, stop=True).then_inc(s_wqk, 1)
            turn_x(0)
            warm(WARM[1])
            pe.wait_ge(s_wqk_sb, 1)
            query(0)
            turn_x(1)
            warm(WARM[2])
            for b in range(BATCHES):
                for qt in range(QT):
                    before, after = pairs_of(b, qt)
                    score(b, qt, 0)
                    if b == 0 and qt == 0:
                        query(1)
                    score(b, qt, 1)
                    for g in before:
                        unit(g)
                    if b == 1 and qt == 1:
                        turn_x(2)
                    if b == 3 and qt == 0:
                        logits(0)
                    score(b, qt, 2)
                    for n, g in enumerate(after):
                        unit(g)
                        if n == 0 and b == 1 and qt == 1:
                            query(2)
                        if n == 1 and b >= 2:
                            attend(b - 2) if qt == 0 else turn_y(b - 2)
            first = PAIRS * (BATCHES - 1)
            unit(first)
            logits(1)
            unit(first + 1)
            up(0)
            unit(first + 2)
            attend(2)
            unit(first + 3)
            up(1)
            unit(first + 4)
            unit(first + 5)
            turn_y(2)
            unit(first + 6)
            weigh(first + 5)
            weigh(first + 6)
            logits(2)
            turn_comb(0)
            up(2)
            spread_weights(1)
            spread_weights(2)
            attend(3)
            for i in range(3, STEPS + LAG):
                if i < STEPS:
                    up(i)
                if i == LOGITS3:
                    logits(3)
                if i == FT + 1:
                    turn_comb(1)
                elif i < STEPS - 1:
                    spread_weights(i)
                if i == TURN_Y3:
                    turn_y(3)
                down(i - LAG)
                if i == FT + 1:
                    spread_weights(i)


def kernel(**inputs):
    import numpy as np
    import concourse.bacc as bacc
    from concourse.bass_utils import run_bass_kernel_spmd

    a = {k: np.asarray(v) for k, v in inputs.items()}
    ctx = a["ctx_1024"]
    full = FULL_KT * P
    arrays = {
        "x": a["x"].reshape(TILES, P, D).transpose(1, 0, 2).reshape(P, TILES * D),
        "ctxT": ctx.transpose(0, 2, 1),
        "ctxN": ctx[:, :full].reshape(BATCHES, FULL_KT, P, D).transpose(0, 2, 1, 3).reshape(BATCHES, P, full),
        "ctxTail": ctx[:, full:],
        "wq": a["L0_xattn_Wq"],
        "wk": a["L0_xattn_Wk"],
        "wvT": a["L0_xattn_Wv"].T,
        "wgT": a["L0_ffn_w_gate"].T,
        "w1T": np.concatenate([a["L0_ffn_w1_e"].reshape(-1, D).T, a["L0_ffn_w1_s"].T], axis=1),
        "w3T": np.concatenate([a["L0_ffn_w3_e"].reshape(-1, D).T, a["L0_ffn_w3_s"].T], axis=1),
        "w2T": np.concatenate([a["L0_ffn_w2_e"].transpose(0, 2, 1).reshape(-1, D), a["L0_ffn_w2_s"].T], axis=0)
                 .reshape(FT, P, D).transpose(1, 0, 2).reshape(P, FT * D),
        "g_xattn": a["g_xattn"].reshape(1, 1),
        "g_ffn": a["g_ffn"].reshape(1, 1),
    }
    arrays = {f"in_{k}": np.ascontiguousarray(v) for k, v in arrays.items()}
    nc = bacc.Bacc("TRN2", target_bir_lowering=False, num_devices=1)
    args = [nc.dram_tensor(k, v.shape, mybir.dt.from_np(v.dtype), kind="ExternalInput").ap()
            for k, v in arrays.items()]
    args.append(nc.dram_tensor("out_T", (D, TOKENS), F32, kind="ExternalOutput").ap())
    build(nc, *args)
    r = run_bass_kernel_spmd(nc, [arrays], core_ids=[0])
    return r.results[0]["out_T"].T.reshape(BATCHES, SEQ, D)
```
